# Optimizing a Trainium2 kernel written in Bass

```python
import numpy as np
import jax
import jax.numpy as jnp

def _softmax(x, axis=-1):
    return jax.nn.softmax(x, axis=axis)

def _gelu(x):
    return jax.nn.gelu(x, approximate=True)

def _silu(x):
    return jax.nn.silu(x)

def _sigmoid(x):
    return jax.nn.sigmoid(x)

def _layernorm(x, axis=-1, eps=1e-05):
    m = jnp.mean(x, axis=axis, keepdims=True)
    v = jnp.var(x, axis=axis, keepdims=True)
    return (x - m) / jnp.sqrt(v + eps)

def _scatter_add(tgt, idx, src, axis=0):
    return tgt.at[idx].add(src)

def _segment_sum(src, seg, n):
    return jax.ops.segment_sum(src, seg, n)
kernel_name = 'mk_prb_d1_jaxref_r8_a6505d'

def setup_inputs(seed: int=0):
    np.random.seed(seed)
    _w = jnp.asarray

    def _L0_attn_setup():
        import jax, jax.numpy as jnp
        import numpy as np
        B, N, D, H, C = (4, 1024, 128, 16, 128)
        HD = D // H
        THRESHOLD = 0.99

        def _chunk_scan(qc, kc, vc, lf):
            mask = jnp.tril(jnp.ones((C, C), bool))

            def step(S, inputs):
                qb, kb, vb, lb = inputs
                o_inter = jnp.einsum('bhid,bhde->bhie', qb * jnp.exp(lb)[..., None], S)
                A = jnp.einsum('bhid,bhjd->bhij', qb, kb)
                diff = jnp.where(mask, lb[..., :, None] - lb[..., None, :], -jnp.inf)
                A = A * jnp.exp(diff)
                o_intra = jnp.einsum('bhij,bhjd->bhid', A, vb)
                tot = lb[..., -1]
                kd = kb * jnp.exp(tot[..., None, None] - lb[..., None])
                S_new = jnp.exp(tot)[..., None, None] * S + jnp.einsum('bhjd,bhje->bhde', kd, vb)
                return (S_new, o_inter + o_intra)
            S0 = jnp.zeros((qc.shape[1], H, HD, HD), qc.dtype)
            _, o = jax.lax.scan(step, S0, (qc, kc, vc, lf))
            return o
        key = jax.random.key(seed)
        ks = jax.random.split(key, 6)
        std = 0.02
        return {'x': jax.random.normal(ks[0], (B, N, D), jnp.float32), 'Wq': jax.random.normal(ks[1], (D, D), jnp.float32) * std, 'Wk': jax.random.normal(ks[2], (D, D), jnp.float32) * std, 'Wv': jax.random.normal(ks[3], (D, D), jnp.float32) * std, 'Wo': jax.random.normal(ks[4], (D, D), jnp.float32) * std, 'Wf': jax.random.normal(ks[5], (H, D), jnp.float32) * std, 'delta': jnp.full((H,), float(np.log(THRESHOLD / (1.0 - THRESHOLD))), jnp.float32), 'norm_weight': jnp.ones((D,), jnp.float32)}
    _L0_attn_in = _L0_attn_setup()

    def _L0_ffn_setup():
        import jax, jax.numpy as jnp
        import numpy as np
        NUM_EXPERTS = 8
        TOP_K = 2
        FIXED_IDX = 0
        D_MODEL = 128
        D_FF = 512
        B, S = (4, 256)

        def _route(flat_x, Wr):
            logits = flat_x @ Wr.T
            probs = jax.nn.softmax(logits.astype(jnp.float32), axis=-1).astype(flat_x.dtype)
            fixed_probs = probs[:, FIXED_IDX:FIXED_IDX + 1]
            remaining = probs[:, 1:]
            other_probs, other_local = jax.lax.top_k(remaining, TOP_K - 1)
            other_idx = other_local + 1
            topk_idx = jnp.concatenate([jnp.full((flat_x.shape[0], 1), FIXED_IDX, dtype=jnp.int32), other_idx], axis=1)
            topk_probs = jnp.concatenate([fixed_probs, other_probs], axis=1)
            topk_probs = topk_probs / jnp.clip(topk_probs.sum(axis=-1, keepdims=True), 1e-09)
            gates = jnp.sum(jax.nn.one_hot(topk_idx, NUM_EXPERTS, dtype=topk_probs.dtype) * topk_probs[..., None], axis=1)
            return gates
        key = jax.random.key(seed)
        ks = jax.random.split(key, 5)
        scale_r = 1.0 / np.sqrt(D_MODEL)
        return {'x': jax.random.normal(ks[0], (B, S, D_MODEL), dtype=jnp.float32), 'Wr': jax.random.normal(ks[1], (NUM_EXPERTS, D_MODEL), dtype=jnp.float32) * scale_r, 'W1': jax.random.normal(ks[2], (NUM_EXPERTS, D_FF, D_MODEL), dtype=jnp.float32) * scale_r, 'W2': jax.random.normal(ks[3], (NUM_EXPERTS, D_MODEL, D_FF), dtype=jnp.float32) * (1.0 / np.sqrt(D_FF)), 'W3': jax.random.normal(ks[4], (NUM_EXPERTS, D_FF, D_MODEL), dtype=jnp.float32) * scale_r}
    _L0_ffn_in = _L0_ffn_setup()
    _d = {'L0_attn_x': _L0_attn_in['x'], 'L0_attn_Wq': _L0_attn_in['Wq'], 'L0_attn_Wk': _L0_attn_in['Wk'], 'L0_attn_Wv': _L0_attn_in['Wv'], 'L0_attn_Wo': _L0_attn_in['Wo'], 'L0_attn_Wf': _L0_attn_in['Wf'], 'L0_attn_delta': _L0_attn_in['delta'], 'L0_attn_norm_weight': _L0_attn_in['norm_weight'], 'L0_ffn_Wr': _L0_ffn_in['Wr'], 'L0_ffn_W1': _L0_ffn_in['W1'], 'L0_ffn_W2': _L0_ffn_in['W2'], 'L0_ffn_W3': _L0_ffn_in['W3']}
    _x0 = _d['L0_attn_x']
    _d['L0_attn_x'] = jax.random.normal(jax.random.fold_in(jax.random.key(seed), 1), (2, 2048, 128), dtype=_x0.dtype)
    del _x0
    return _d

def reference(L0_attn_x, L0_attn_Wq, L0_attn_Wk, L0_attn_Wv, L0_attn_Wo, L0_attn_Wf, L0_attn_delta, L0_attn_norm_weight, L0_ffn_Wr, L0_ffn_W1, L0_ffn_W2, L0_ffn_W3):

    def _L0_attn_ref(x, Wq, Wk, Wv, Wo, Wf, delta, norm_weight):
        import jax, jax.numpy as jnp
        import numpy as np
        B, N, D, H, C = (4, 1024, 128, 16, 128)
        HD = D // H
        THRESHOLD = 0.99

        def _chunk_scan(qc, kc, vc, lf):
            mask = jnp.tril(jnp.ones((C, C), bool))

            def step(S, inputs):
                qb, kb, vb, lb = inputs
                o_inter = jnp.einsum('bhid,bhde->bhie', qb * jnp.exp(lb)[..., None], S)
                A = jnp.einsum('bhid,bhjd->bhij', qb, kb)
                diff = jnp.where(mask, lb[..., :, None] - lb[..., None, :], -jnp.inf)
                A = A * jnp.exp(diff)
                o_intra = jnp.einsum('bhij,bhjd->bhid', A, vb)
                tot = lb[..., -1]
                kd = kb * jnp.exp(tot[..., None, None] - lb[..., None])
                S_new = jnp.exp(tot)[..., None, None] * S + jnp.einsum('bhjd,bhje->bhde', kd, vb)
                return (S_new, o_inter + o_intra)
            S0 = jnp.zeros((qc.shape[1], H, HD, HD), qc.dtype)
            _, o = jax.lax.scan(step, S0, (qc, kc, vc, lf))
            return o
        b, n, d = x.shape
        q = jax.nn.silu(x @ Wq.T)
        k = jax.nn.silu(x @ Wk.T)
        v = x @ Wv.T
        log_f = jax.nn.log_sigmoid(x @ Wf.T + delta)
        nc = n // C

        def to_chunks(t):
            return t.reshape(b, nc, C, H, HD).transpose(1, 0, 3, 2, 4)
        qc, kc, vc = map(to_chunks, (q, k, v))
        lf = jnp.cumsum(log_f.reshape(b, nc, C, H).transpose(1, 0, 3, 2), axis=-1)
        o = _chunk_scan(qc, kc, vc, lf)
        o = o.transpose(1, 0, 3, 2, 4).reshape(b, n, d)
        o = o * jax.lax.rsqrt(jnp.mean(o * o, axis=-1, keepdims=True) + 1e-06) * norm_weight
        return o @ Wo.T

    def _L0_ffn_ref(x, Wr, W1, W2, W3):
        import jax, jax.numpy as jnp
        import numpy as np
        NUM_EXPERTS = 8
        TOP_K = 2
        FIXED_IDX = 0
        D_MODEL = 128
        D_FF = 512
        B, S = (4, 256)

        def _route(flat_x, Wr):
            logits = flat_x @ Wr.T
            probs = jax.nn.softmax(logits.astype(jnp.float32), axis=-1).astype(flat_x.dtype)
            fixed_probs = probs[:, FIXED_IDX:FIXED_IDX + 1]
            remaining = probs[:, 1:]
            other_probs, other_local = jax.lax.top_k(remaining, TOP_K - 1)
            other_idx = other_local + 1
            topk_idx = jnp.concatenate([jnp.full((flat_x.shape[0], 1), FIXED_IDX, dtype=jnp.int32), other_idx], axis=1)
            topk_probs = jnp.concatenate([fixed_probs, other_probs], axis=1)
            topk_probs = topk_probs / jnp.clip(topk_probs.sum(axis=-1, keepdims=True), 1e-09)
            gates = jnp.sum(jax.nn.one_hot(topk_idx, NUM_EXPERTS, dtype=topk_probs.dtype) * topk_probs[..., None], axis=1)
            return gates
        batch, seq, d_model = x.shape
        flat_x = x.reshape(batch * seq, d_model)
        gates = _route(flat_x, Wr)
        out = jnp.zeros_like(flat_x)
        for e in range(NUM_EXPERTS):
            h = jax.nn.silu(flat_x @ W1[e].T) * (flat_x @ W3[e].T)
            out = out + gates[:, e:e + 1] * (h @ W2[e].T)
        return out.reshape(batch, seq, d_model)
    x = L0_attn_x
    xn = _layernorm(x, axis=-1)
    x = x + _L0_attn_ref(xn, L0_attn_Wq, L0_attn_Wk, L0_attn_Wv, L0_attn_Wo, L0_attn_Wf, L0_attn_delta, L0_attn_norm_weight) + _L0_ffn_ref(xn, L0_ffn_Wr, L0_ffn_W1, L0_ffn_W2, L0_ffn_W3)
    return x

_drawn_inputs = setup_inputs


def setup_inputs(seed=0):
    import zlib

    import numpy as np

    out = dict(_drawn_inputs(seed))
    spreads = {'L0_attn_delta': (4.595119953155518, 0.2), 'L0_attn_norm_weight': (1.0, 0.2)}
    factors = {'L0_attn_Wf': 8.0}
    for name, (base, spread) in spreads.items():
        noise = np.random.default_rng([zlib.crc32(name.encode()), seed]).standard_normal(out[name].shape)
        drawn = base * np.exp(spread * noise) if base else spread * noise
        out[name] = jnp.asarray(drawn.astype(out[name].dtype))
    for name, factor in factors.items():
        out[name] = (out[name] * factor).astype(out[name].dtype)
    return out
```

```python
from contextlib import ExitStack

import numpy as np
import concourse.bass as bass
from concourse import mybir

F32 = mybir.dt.float32
F16 = mybir.dt.float16
BF16 = mybir.dt.bfloat16
I32 = mybir.dt.int32
ALU = mybir.AluOpType
ACT = mybir.ActivationFunctionType
AX_X = mybir.AxisListType.X

P = 128
BATCH, SEQ, D = 2, 2048, 128
TOK = BATCH * SEQ
NCH = TOK // P
CPB = NCH // BATCH
H, HD = 16, 8
SUB = 64
NS = P // SUB
E, FF = 8, 512
FB = FF // P
R = E - 1
GRP = 4
NGRP = NCH // GRP
NBLK = NCH + R - 1
ROW = D + 1
LN_EPS, RMS_EPS = 1e-5, 1e-6
WS = 64.0
QS = 2.0 * WS
OS = QS * QS * WS
BIG = -1.0e30
DROWS = 3 * H + 3 * NS + SUB
NLB, NSEL = 3 * H, 3 * NS

COLS = {}
_at = 0
for _name, _n in [("rank", P), ("ones", P), ("cum", P), ("suffix", P), ("ident", P), ("expand", P),
                  ("scan0", R * NCH), ("one7", R), ("order", R), ("fill", NCH), ("blk", NBLK),
                  ("hmask", H), ("smask", NS)]:
    COLS[_name] = (_at, _at + _n)
    _at += _n
NCONST = _at


def constants():
    k = np.arange(P)[:, None]
    m = np.arange(P)[None, :]
    same = (k // SUB) == (m // SUB)
    c = np.zeros((P, NCONST), np.float32)

    def put(name, v):
        a, b = COLS[name]
        c[:, a:b] = v

    put("rank", k < m)
    put("ones", 1)
    put("cum", (k <= m) & same)
    put("suffix", (k > m) & same)
    put("ident", k == m)
    put("expand", (k % 32 == m // HD))
    put("scan0", (np.arange(R * NCH) % NCH != 0)[None])
    put("one7", 1)
    put("order", (R - np.arange(R))[None])
    put("fill", (P * np.arange(NCH))[None])
    put("blk", np.arange(NBLK)[None])
    put("hmask", k // HD == np.arange(H)[None])
    put("smask", k // SUB == np.arange(NS)[None])
    return c


def decay_constants():
    j = np.arange(P)
    left = np.zeros((NSEL + SUB, P), np.float32)
    for p in range(3):
        for s in range(NS):
            left[p * NS + s] = (j // SUB == s)
    left[NSEL:] = (np.arange(SUB)[:, None] == (j % SUB)[None])
    right = np.zeros((DROWS, H, SUB), np.float32)
    for p in range(3):
        for h in range(H):
            right[p * H + h, h] = -1
    right[NLB + NSEL:] = np.where(np.arange(SUB)[None, None, :] < np.arange(SUB)[:, None, None], BIG, 0)


    def bits(a):
        return (np.ascontiguousarray(a).view(np.uint32) >> 16).astype(np.uint16)

    return bits(left), bits(right.reshape(DROWS, H * SUB))



def build(nc, x, wqkv, wo, wrf, delta, nw, w13, w2, const, dleft, dright, out,
          qk_scr, lb_scr, xsort, ytok):
    dleft, dright = dleft.bitcast(BF16), dright.bitcast(BF16)
    with ExitStack() as ctx:
        def sb(name, shape, dt=F32):
            return ctx.enter_context(nc.sbuf_tensor(name, shape, dt))

        def sem(name):
            return ctx.enter_context(nc.semaphore(name))

        def wait(eng, s, value):
            if isinstance(value, int) and value <= 0:
                return
            eng.wait_ge(s, value)

        def at(eng, value):
            return value if isinstance(value, int) else eng.snap(value)

        def loop(eng, count, body, peel=1):
            for i in range(peel):
                body(i)
            if peel < count:
                with eng.Fori(peel, count) as i:
                    body(i)

        class Region:

            def __init__(self, name, kib):
                self.tensor, self.at, self.size = sb(name, [P, kib * 256]), 0, kib * 256

            def take(self, shape, dt=F32):
                per = 1 if dt in (F32, I32) else 2
                n = int(np.prod(shape[1:]))
                words = -(-n // per)
                a = self.at
                self.at += words
                assert self.at <= self.size, (self.at, self.size)
                v = self.tensor[0:shape[0], a:a + words]
                if dt != F32:
                    v = v.bitcast(dt)
                names = "abcd"[:len(shape) - 1]
                if len(shape) > 2:
                    v = v.rearrange(f"p ({' '.join(names)}) -> p {' '.join(names)}",
                                    **{k: m for k, m in zip(names[1:], shape[2:])})
                return v

            def again(self, at=0):
                self.at = at

        PS = ctx.enter_context(nc.psum_tensor("PS", [P, 8, 512], F32))
        cst = sb("cst", [P, NCONST])

        def cc(name):
            a, b = COLS[name]
            return cst[:, a:b]

        x_sb = sb("x_sb", [P, NCH, D])
        rows = sb("rows", [P, NCH, ROW])
        attn = rows[:, :, 0:D]
        xh = sb("xh", [P, TOK], F16)
        xl = sb("xl", [P, TOK], F16)
        w13h = sb("w13h", [P, E, 2, 2, FF], F16)
        elb = sb("elb", [P, NCH, H])
        sdec = sb("sdec", [P, NCH, H])
        dec = sb("dec", [P, NCH * NS])
        lf = sb("lf", [P, (NCH + 1) * H])
        small = sb("small", [P, 12, NCH])
        mean_var = sb("mean_var", [P, 2, GRP, 2])
        stats = sb("stats", [P, 2, GRP, 6])
        g0, g1, ssq, sdv, rstd = (small[:, k, :] for k in range(5))
        rmax, rsum, ptop, den, den2, oscore, slot = (small[:, k, :] for k in range(5, 12))
        slot_i = sb("slot_i", [P, NCH], I32)
        expert = sb("expert", [1, NBLK], I32)
        ids = sb("ids", [P, NBLK], I32)
        eps = sb("eps", [P, 3])
        eps_ln, eps_rms, one = eps[:, 0:1], eps[:, 1:2], eps[:, 2:3]
        wrf_sb = sb("wrf_sb", [P, E + H])
        delta_sb = sb("delta_sb", [P, H])
        nw_sb = sb("nw_sb", [P, 1])
        wo_sb = sb("wo_sb", [P, D])
        wqh = sb("wqh", [P, 3 * D], F16)
        wql = sb("wql", [P, 3 * D], F16)

        Z = Region("Z", 48)
        wraw = Z.take([P, 3, D])
        wo_raw = Z.take([P, D])
        rl = Z.take([P, NCH, E])
        rexp = Z.take([P, NCH, E])
        eq = Z.take([P, NCH, R])
        oh = Z.take([P, NCH, R])
        tt = Z.take([P, R, NCH])
        incl = Z.take([P, R, NCH])
        off = Z.take([P, R, NCH])
        bcmp = Z.take([1, NBLK, R - 1])
        bsum = Z.take([1, NBLK])
        nblk = Z.take([P, 3, R])
        zf = Z.take([P, NCH, H])
        zm = Z.take([P, NCH, H])
        ze = Z.take([P, NCH, H])
        lbT = Z.take([P, 8 * P])
        lbS = Z.take([P, 3, 8 * P], BF16)
        wstage = Z.take([P, 2, 2, FF])
        Z.again()
        qT = Z.take([P, TOK])
        k2 = Z.take([P, NCH, D])
        v_sb = Z.take([P, NCH, D])
        Z.again()
        w2_sb = Z.take([P, E, FB, D])

        C = Region("C", 44)
        xnT = C.take([P, 2, GRP * P])
        zero = C.take([P, NBLK, ROW])
        C.again()
        tq = C.take([P, 2, 2, GRP * P])
        tk = C.take([P, 2, GRP, P])
        kT = C.take([P, 2, GRP * P])
        qkh = C.take([P, 2, 2, GRP * P], F16)
        qkl = C.take([P, 2, 2, GRP * P], F16)
        C.again()
        q_st = C.take([3 * HD, 2, H, P], F16)
        k_st = C.take([3 * HD, 2, H, P], F16)
        ebuf = C.take([P, 2, H * SUB])
        pbuf = C.take([P, 2, H * SUB])
        kd = C.take([P, 2, D])
        v2 = C.take([P, 2, H * NS * HD])
        um = C.take([P, 2, NS, D])
        state = C.take([P, 2, NS, D])
        q_now = C.take([P, 2, P])
        o1 = C.take([P, D])
        o_sb = C.take([P, 2, D])
        junk = C.take([P, 2, D])
        oT = C.take([P, 2, D])
        C.again()
        xrow = C.take([P, 2, ROW])
        xsh = C.take([P, 2, P], F16)
        xsl = C.take([P, 2, P], F16)
        silu = C.take([P, 2, FF])
        hid = C.take([P, 2, FF])
        ysb = C.take([P, 2, D])
        yt = C.take([P, 2, D])
        t1 = C.take([P, 2, D])
        t2 = C.take([P, 2, D])
        osb = C.take([P, 2, D])
        dL = sb("dL", [DROWS, NCH, P], BF16)
        dR = sb("dR", [DROWS, 2, H * SUB], BF16)

        class Sems(dict):
            def __missing__(self, name):
                self[name] = sem(name)
                return self[name]

        S = Sems()
        NCONSTDMA = 6

        lg = PS[:, 2:4, :].rearrange("p b (c n) -> p (b c) n", n=2 * 512 // NCH)
        rank_ps = PS[:, 4, 0:NCH * R].rearrange("p (c e) -> p c e", e=R)
        ntok_ps = PS[:, 4, NCH * R:2 * NCH * R].rearrange("p (c e) -> p e c", e=R)

        def chunk(i, b, k=0):
            return ((b - k) % 2) * CPB + i + (b - k) // 2

        block = ctx.enter_context(nc.Block())

        @block.sync
        def _(sp):
            def load_x(i):
                for u in range(2):
                    g = 2 * i + u
                    gs = bass.ds(at(sp, g * GRP), GRP)
                    wait(sp, S[f"x_in{u}"], 16 * i)
                    sp.dma_start(x_sb[:, gs, :], x.rearrange("(c p) d -> p c d", p=P)[:, gs, :]
                                 ).then_inc(S[f"x_in{u}"], 16)

            loop(sp, NGRP // 2, load_x)

            def load_w(i):
                for u in range(2):
                    e = at(sp, 2 * i + u)
                    wait(sp, S["w_lo"], 2 * i + u - 1)
                    sp.dma_start(wstage[:, u, :, :], w13[:, bass.ds(e, 1)].rearrange("p o w f -> p (o w) f")
                                 ).then_inc(S[f"stage_in{u}"], 16)

            loop(sp, E // 2, load_w)

            sp.wait_ge(S["lb_parts"], 3)
            for k in range(4):
                for p in range(3):
                    src = lbS[32 * k:32 * k + H, p, :]
                    sp.dma_start(dL[p * H:(p + 1) * H, 8 * k:8 * k + 8, :], src.rearrange("p (c t) -> p c t", t=P)
                                 ).then_inc(S["lb_moved"], 16)
                    for s in range(NS):
                        sp.dma_start(lb_scr[8 * k:8 * k + 8, p, s].rearrange("c h i -> h c i"),
                                     src.rearrange("p (c s i) -> p c s i", s=NS, i=SUB)[:, :, s, :]
                                     ).then_inc(S["lb_moved"], 16)

            def store_parts(i):
                for u in range(2):
                    g = 2 * i + u
                    cols = bass.ds(at(sp, g * GRP * P), GRP * P)
                    sp.wait_ge(S["qk_hi"], 2 * g + 2)
                    sp.wait_ge(S["qk_lo"], 2 * g + 2)
                    for t in range(2):
                        for p, src in enumerate([qkh, qkl, qkh] if t == 0 else [qkh, qkh, qkl]):
                            sp.dma_start(
                                qk_scr[t, p].rearrange("d h t -> h d t")[:, :, cols],
                                src[:, u, t, :]).then_inc(S[f"qk_out{u}"], 16)

            loop(sp, NGRP // 2, store_parts)

            sp.wait_ge(S["lb_moved"], 16 * 36)
            for u in range(2):
                sp.wait_ge(S[f"qk_out{u}"], 16 * 6 * (NGRP // 2))

            def load_stacks(i):
                for b in range(2):
                    n, c = 2 * i + b, chunk(i, b)
                    tok, cs = bass.ds(at(sp, c * P), P), bass.ds(at(sp, c), 1)
                    wait(sp, S["pe_a"], n - 1)
                    wait(sp, S["pe_d"], n - 1)
                    wait(sp, S["pe_i"], n - 1)
                    sp.dma_start(q_now[:, b, :], qT[:, tok]).then_inc(S[f"q_in{b}"], 16)
                    sp.dma_start(dR[NLB:NLB + NSEL, b, :],
                                 lb_scr[cs].rearrange("o p s h i -> (o p s) (h i)")
                                 ).then_inc(S[f"dr_in{b}"], 16)
                    for t, dst in ((0, q_st), (1, k_st)):
                        sp.dma_start(dst[:, b, :, :],
                                     qk_scr[t].rearrange("p d h t -> (p d) h t")[:, :, tok]
                                     ).then_inc(S[f"st_in{b}"], 16)

            loop(sp, CPB, load_stacks)

            sp.wait_ge(S["pe_i"], NCH)
            sp.wait_ge(S["pool_v2"], NCH)
            sp.dma_start(w2_sb, w2).then_inc(S["w2_in"], 16)
            for b in range(2):
                sp.wait_ge(S[f"scattered{b}"], 16 * CPB)
            sp.wait_ge(S["pe_w"], NCH)
            sp.wait_ge(S["act_ss"], NCH)

            def load_rows(i):
                for u in range(2):
                    n = 2 * i + u
                    tok = bass.ds(at(sp, n * P), P)
                    wait(sp, S["xs_ps"], n - 1)
                    wait(sp, S["id_copied"], n - 1)
                    sp.dma_start(xrow[:, u, :], xsort[tok, :]).then_inc(S[f"xrow_in{u}"], 16)

            loop(sp, NBLK // 2, load_rows)

            for u in range(2):
                sp.wait_ge(S[f"y_out{u}"], 16 * (NBLK // 2))

            def load_y(i, u):
                tok = bass.ds(at(sp, (2 * i + u) * P), P)
                wait(sp, S["dve_t2"], 2 * i + u - 1)
                sp.dma_start(yt[:, u, :], ytok[tok, :]).then_inc(S[f"yt_in{u}"], 16)

            def store_out(i, u):
                tok = bass.ds(at(sp, (2 * i + u) * P), P)
                sp.wait_ge(S["dve_out"], 2 * i + u + 1)
                sp.dma_start(out[tok, :], osb[:, u, :]).then_inc(S[f"stored{u}"], 16)

            for u in range(2):
                load_y(0, u)

            def move(i):
                for u in range(2):
                    load_y(i + 1, u)
                    store_out(i, u)

            loop(sp, NCH // 2 - 1, move)
            for u in range(2):
                store_out(NCH // 2 - 1, u)
            for u in range(2):
                sp.wait_ge(S[f"stored{u}"], 16 * (NCH // 2))

        @block.gpsimd
        def _(pool):
            pool.memset(zero, 0.0).then_inc(S["pool_init"], 1)
            pool.iota(rows[:, :, D].bitcast(I32), pattern=[[P, NCH]], base=0, channel_multiplier=1
                      ).then_inc(S["pool_init"], 1)
            pool.wait_ge(S["pool_init"], 2)
            pool.iota(zero[:, :, D].bitcast(I32), pattern=[[1, NBLK]], base=TOK, channel_multiplier=NBLK
                      ).then_inc(S["pool_init"], 1)
            pool.wait_ge(S["pool_init"], 3)
            pool.dma_start(xsort.rearrange("(p n) r -> p n r", n=NBLK), zero).then_inc(S["init_out"], 16)

            def low(i):
                for u in range(2):
                    g = 2 * i + u
                    cols = bass.ds(g * GRP * P, GRP * P)
                    pool.wait_ge(S["xnT_sb"], g + 1)
                    pool.wait_ge(S["xh_ready"], g + 1)
                    pool.tensor_tensor(xl[:, cols], xnT[:, u, :], xh[:, cols], ALU.subtract).then_inc(S["xl_ready"], 1)

            loop(pool, NGRP // 2, low)

            pool.wait_ge(S["const_in"], 16 * NCONSTDMA)
            pool.wait_ge(S["init_out"], 16)
            pool.wait_ge(S["slots"], 1)
            for n in range(NCH):
                b, c = n % 2, chunk(n // 2, n % 2)
                wait(pool, S[f"scattered{b}"], 16 * (n // 2))
                pool.indirect_dma_start(xsort, bass.IndirectOffsetOnAxis(ap=slot_i[:, c:c + 1], axis=0),
                                        rows[:, c, :], None).then_inc(S[f"scattered{b}"], 16)
                if n == 0:
                    pool.wait_ge(S["decays"], 3)
                    pool.wait_ge(S["k2_ready"], NGRP)
                    pool.wait_ge(S["v_ready"], NGRP)
                    pool.wait_ge(S["qk_lo"], 2 * NGRP)
                    for u in range(2):
                        pool.wait_ge(S[f"qk_out{u}"], 16 * 6 * (NGRP // 2))
                wait(pool, S["pe_u"], n - 1)
                pool.tensor_tensor(kd[:, b, :].rearrange("p (h d) -> p h d", d=HD),
                                   k2[:, c, :].rearrange("p (h d) -> p h d", d=HD),
                                   sdec[:, c, :].unsqueeze(2).broadcast_to([P, H, HD]),
                                   ALU.mult).then_inc(S["pool_kd"], 1)
                wait(pool, S["pe_av"], n - 1)
                pool.tensor_tensor(v2[:, b, :].rearrange("p (h s e) -> p h s e", s=NS, e=HD),
                                   v_sb[:, c, :].rearrange("p (h e) -> p h e", e=HD).unsqueeze(2)
                                   .broadcast_to([P, H, NS, HD]),
                                   cc("smask").unsqueeze(1).unsqueeze(3).broadcast_to([P, H, NS, HD]),
                                   ALU.mult).then_inc(S["pool_v2"], 1)

            for n in range(NBLK):
                pool.wait_ge(S["y_sb"], n + 1)
                pool.wait_ge(S["id_copied"], n + 1)
                pool.indirect_dma_start(ytok, bass.IndirectOffsetOnAxis(ap=ids[:, n:n + 1], axis=0),
                                        ysb[:, n % 2, :], None).then_inc(S[f"y_out{n % 2}"], 16)

        @block.scalar
        def _(act):
            for dst, src in ((cst[:], const), (wrf_sb[:], wrf), (delta_sb[:], delta.partition_broadcast(P)),
                             (nw_sb[:], nw), (wo_raw, wo), (wraw, wqkv)):
                act.dma_start(dst, src).then_inc(S["const_in"], 16)
            for b in range(2):
                act.dma_start(dR[0:NLB, b, :], dright[0:NLB, :]).then_inc(S["dstat_in"], 16)
                act.dma_start(dR[NLB + NSEL:DROWS, b, :], dright[NLB + NSEL:DROWS, :]).then_inc(S["dstat_in"], 16)
            act.dma_start(dL[NLB:DROWS, :, :], dleft.unsqueeze(1).broadcast_to([NSEL + SUB, NCH, P])
                          ).then_inc(S["dstat_in"], 16)

            act.wait_ge(S["eps_set"], 3)

            def transposed(i):
                for u in range(2):
                    g = 2 * i + u
                    gs = bass.ds(g * GRP, GRP)
                    act.wait_ge(S["ln_aggr"], g + 1)
                    act.activation(sdv[:, gs], mean_var[:, u, :, 1], ACT.Sqrt, bias=eps_ln).then_inc(S["ln_sd"], 1)
                    act.wait_ge(S["xnT_ps"], g + 1)
                    wait(act, S["logits_ready"], g - 1)
                    wait(act, S["xl_ready"], g - 1)
                    act.activation(xnT[:, u, :], PS[:, u, :], ACT.Copy).then_inc(S["xnT_sb"], 1)
                    act.activation(xh[:, bass.ds(g * GRP * P, GRP * P)], PS[:, u, :], ACT.Copy).then_inc(S["xh_ready"], 1)

            loop(act, NGRP // 2, transposed)

            act.wait_ge(S["const_in"], 16 * NCONSTDMA)
            act.activation(wqh[:], wraw.rearrange("p w d -> p (w d)"), ACT.Copy, scale=WS).then_inc(S["wq_hi"], 1)

            act.wait_ge(S["forget_abs"], 1)
            act.activation(ze, ze, ACT.Exp).then_inc(S["forget_exp"], 1)
            act.wait_ge(S["forget_exp"], 1)
            act.activation(ze, ze, ACT.Ln, bias=one).then_inc(S["forget_ln"], 1)
            act.wait_ge(S["router_in"], 1)
            act.activation(rexp, rl, ACT.Exp).then_inc(S["router_exp"], 1)
            act.wait_ge(S["cum_ps"], 1)
            act.activation(elb[:].rearrange("p c h -> p (c h)"), PS[:, 5, :], ACT.Exp).then_inc(S["decays"], 1)
            act.activation(sdec[:].rearrange("p c h -> p (c h)"), PS[:, 6, :], ACT.Exp).then_inc(S["decays"], 1)
            act.wait_ge(S["lbT_ps"], 1)
            act.activation(lbT, PS[:, 0:2, :].rearrange("p b n -> p (b n)"), ACT.Copy).then_inc(S["lbT_sb"], 1)
            act.wait_ge(S["tot_ps"], 1)
            act.activation(dec[:].rearrange("p (k n) -> p k n", k=4), PS[:, 0:4, 0:NCH * NS // 4], ACT.Exp
                           ).then_inc(S["decays"], 1)

            def high_w(i):
                for u in range(2):
                    act.wait_ge(S[f"stage_in{u}"], 16 * i + 16)
                    act.activation(w13h[:, bass.ds(2 * i + u, 1), :, 0, :].rearrange("p o w f -> p (o w) f"),
                                   wstage[:, u, :, :], ACT.Copy, scale=WS).then_inc(S["w_hi"], 1)

            loop(act, E // 2, high_w)

            def project(i):
                for u in range(2):
                    g = 2 * i + u
                    act.wait_ge(S["q_ps"], g + 1)
                    wait(act, S["qk_f32"], 2 * g - 2)
                    for t in range(2):
                        last = act.activation(tq[:, u, t, :], PS[:, 4 * u + t, :], ACT.Tanh, scale=0.5 / WS)
                    last.then_inc(S["qk_tanh"], 1)
                    act.wait_ge(S["kv_ps"], g + 1)
                    wait(act, S["k2_ready"], g - 1)
                    kv = PS[:, 4 * u + 2:4 * u + 4, :].rearrange("p b (c n) -> p b c n", n=2 * D)
                    act.activation(tk[:, u].rearrange("p (b c) d -> p b c d", c=2), kv[:, :, :, 0:D], ACT.Tanh,
                                   scale=0.5 / WS).then_inc(S["k_tanh"], 1)
                    act.activation(v_sb[:, bass.ds(g * GRP, GRP), :].rearrange("p (b c) d -> p b c d", c=2),
                                   kv[:, :, :, D:2 * D], ACT.Copy).then_inc(S["v_ready"], 1)
                    act.wait_ge(S["qk_f32"], 2 * g + 2)
                    wait(act, S[f"qk_out{u}"], 16 * 6 * i)
                    wait(act, S["qk_lo"], 2 * g - 2)
                    act.activation(qkh[:, u, 0, :], qT[:, bass.ds(g * GRP * P, GRP * P)], ACT.Copy).then_inc(S["qk_hi"], 1)
                    act.activation(qkh[:, u, 1, :], kT[:, u, :], ACT.Copy).then_inc(S["qk_hi"], 1)

            act.wait_ge(S["lb_moved"], 16 * 36)
            act.wait_ge(S["w_lo"], E)
            act.wait_ge(S["slots"], 1)
            act.wait_ge(S["blocks_known"], 1)
            act.wait_ge(S["xl_ready"], NGRP)
            act.wait_ge(S["init_out"], 16)
            loop(act, NGRP // 2, project)

            def attend(i):
                for b in range(2):
                    n = 2 * i + b

                    def there(k):
                        return not isinstance(n, int) or n - k >= 0

                    if there(3):
                        u = (b - 3) % 2
                        act.wait_ge(S["pe_w"], n - 2)
                        act.wait_ge(S[f"scattered{u}"], 16 * (i + (b - 3) // 2) + 16)
                        act.activation(attn[:, bass.ds(chunk(i, b, 3), 1), :].rearrange("p o d -> p (o d)"),
                                       PS[:, 6 + u, 256:384], ACT.Copy).then_inc(S["act_attn"], 1)
                    if there(2):
                        act.wait_ge(S["pe_t"], n - 1)
                        wait(act, S["pe_w"], n - 3)
                        act.activation(oT[:, b, :], PS[:, 4 + b, 384:512], ACT.Copy).then_inc(S["act_ot"], 1)
                        wait(act, S["act_ss"], n - 3)
                        act.activation(junk[:, b, :], o_sb[:, b, :], ACT.Square,
                                       accum_out=ssq[:, bass.ds(chunk(i, b, 2), 1)]).then_inc(S["act_ss"], 1)
                    if there(0) and not (isinstance(n, int) and n >= NCH):
                        act.wait_ge(S["pe_d"], n + 1)
                        wait(act, S["dve_p"], n - 1)
                        act.activation(ebuf[:, b, :], PS[:, 0:2, :].rearrange("p b n -> p (b n)"), ACT.Exp
                                       ).then_inc(S["act_e"], 1)

            for u in range(2):
                act.wait_ge(S[f"qk_out{u}"], 16 * 6 * (NGRP // 2))
            act.wait_ge(S["qk_lo"], 2 * NGRP)
            act.wait_ge(S["k2_ready"], NGRP)
            loop(act, CPB, attend, peel=2)
            attend(CPB)
            act.wait_ge(S["pe_w"], NCH)
            act.wait_ge(S["scattered1"], 16 * CPB)
            act.activation(attn[:, NCH - 1, :], PS[:, 7, 256:384], ACT.Copy).then_inc(S["act_attn"], 1)
            act.wait_ge(S["act_ss"], NCH)
            act.activation(sdv, ssq, ACT.Sqrt, scale=1.0 / D, bias=eps_rms).then_inc(S["rms_sd"], 1)

            def sorted_hi(n, u):
                act.wait_ge(S["xs_ps"], n + 1)
                wait(act, S["f_b"], n - 1)
                wait(act, S["xs_lo"], n - 1)
                act.activation(xsh[:, u, :], PS[:, 6 + u, 0:P], ACT.Copy).then_inc(S["xs_hi"], 1)

            def silu_of(ph, n, u):
                act.wait_ge(S[ph + "a"], n + 1)
                wait(act, S[ph + "h"], n - 1)
                act.activation(silu[:, u, :], PS[:, u, :], ACT.Silu, scale=1.0 / WS).then_inc(S[ph + "silu"], 1)

            def y_copy(n, u, turn):
                act.wait_ge(S["f_y"], n + 1)
                wait(act, S[f"y_out{u}"], 16 * turn)
                act.activation(ysb[:, u, :], PS[:, 4 + u, 0:D], ACT.Copy).then_inc(S["y_sb"], 1)

            def routed(i):
                for v in range(2):
                    n, u = 2 * i + 1 + v, (1 + v) % 2
                    sorted_hi(n + 1, 1 - u)
                    silu_of("f_", n, u)
                    y_copy(n - 1, 1 - u, i)

            act.wait_ge(S["dve_o"], NCH)
            sorted_hi(0, 0)
            sorted_hi(1, 1)
            silu_of("f_", 0, 0)
            loop(act, NBLK // 2 - 1, routed)
            silu_of("f_", NBLK - 1, 1)
            y_copy(NBLK - 2, 0, NBLK // 2 - 1)
            y_copy(NBLK - 1, 1, NBLK // 2 - 1)

            act.wait_ge(S["f_h"], NBLK)

            def dense(i):
                for u in range(2):
                    silu_of("g_", 2 * i + u, u)

            loop(act, NCH // 2, dense)

        @block.vector
        def _(dve):
            count = {}

            def link(ins, name):
                count[name] = count.get(name, 0) + 1
                ins.then_inc(S[name], 1)
                dve.wait_ge(S[name], count[name])

            dve.memset(eps_ln, LN_EPS).then_inc(S["eps_set"], 1)
            dve.memset(eps_rms, RMS_EPS * OS * OS).then_inc(S["eps_set"], 1)
            dve.memset(one, 1.0).then_inc(S["eps_set"], 1)
            dve.memset(lf[:, NCH * H:], 0.0)

            def norm(i):
                for u in range(2):
                    g = 2 * i + u
                    dve.wait_ge(S[f"x_in{u}"], 16 * i + 16)
                    for j in range(GRP):
                        last = dve.bn_stats(stats[:, u, j, :], x_sb[:, bass.ds(g * GRP + j, 1), :].rearrange("p o d -> p (o d)"))
                    last.then_inc(S["ln_stats"], 1)
                    dve.wait_ge(S["ln_stats"], g + 1)
                    for j in range(GRP):
                        last = dve.bn_aggr(mean_var[:, u, j, :], stats[:, u, j, :])
                    last.then_inc(S["ln_aggr"], 1)
                    gs = bass.ds(g * GRP, GRP)
                    dve.wait_ge(S["ln_sd"], g + 1)
                    dve.reciprocal(rstd[:, gs], sdv[:, gs]).then_inc(S["ln_rstd"], 1)
                    dve.wait_ge(S["ln_rstd"], g + 1)
                    for j in range(GRP):
                        c = bass.ds(g * GRP + j, 1)
                        last = dve.tensor_scalar(rows[:, c, 0:D].rearrange("p o d -> p (o d)"),
                                                 x_sb[:, c, :].rearrange("p o d -> p (o d)"),
                                                 mean_var[:, u, j, 0:1], rstd[:, c], ALU.subtract, ALU.mult)
                    last.then_inc(S["xn_ready"], 1)

            loop(dve, NGRP // 2, norm, peel=NGRP // 2)

            dve.wait_ge(S["logits_ready"], NGRP)
            dve.wait_ge(S["const_in"], 16 * NCONSTDMA)
            link(dve.tensor_tensor(zf, lg[:, :, E:E + H],
                                   delta_sb[:].unsqueeze(1).broadcast_to([P, NCH, H]), ALU.add), "forget")
            link(dve.tensor_scalar(zm, zf, 0.0, None, ALU.min), "forget")
            dve.scalar_tensor_tensor(ze, zm, 2.0, zf, ALU.mult, ALU.subtract).then_inc(S["forget_abs"], 1)
            link(dve.tensor_copy(rl, lg[:, :, 0:E]), "router")
            link(dve.tensor_reduce(rmax, rl, AX_X, ALU.max), "router")
            dve.tensor_tensor(rl, rl, rmax.unsqueeze(2).broadcast_to([P, NCH, E]), ALU.subtract).then_inc(S["router_in"], 1)
            dve.wait_ge(S["forget_ln"], 1)
            dve.tensor_tensor(lf[:, 0:NCH * H], zm.rearrange("p c h -> p (c h)"), ze.rearrange("p c h -> p (c h)"),
                              ALU.subtract).then_inc(S["lf_ready"], 1)
            dve.wait_ge(S["router_exp"], 1)
            dve.tensor_reduce(rsum, rexp, AX_X, ALU.add)
            link(dve.tensor_reduce(ptop, rexp[:, :, 1:E], AX_X, ALU.max), "router")
            dve.tensor_tensor(eq, rexp[:, :, 1:E], ptop.unsqueeze(2).broadcast_to([P, NCH, R]), ALU.is_equal)
            link(dve.tensor_tensor(den, rexp[:, :, 0], ptop, ALU.add), "router")
            link(dve.scalar_tensor_tensor(den2, rsum, 1e-9, den, ALU.mult, ALU.max), "router")
            link(dve.reciprocal(den, den2), "router")
            dve.scalar_tensor_tensor(g0, rexp[:, :, 0], 1.0 / WS, den, ALU.mult, ALU.mult).then_inc(S["gates"], 1)
            dve.scalar_tensor_tensor(g1, ptop, 1.0 / WS, den, ALU.mult, ALU.mult).then_inc(S["gates"], 1)
            link(dve.tensor_tensor(eq, eq, cc("order").unsqueeze(1).broadcast_to([P, NCH, R]), ALU.mult), "router")
            link(dve.tensor_reduce(oscore, eq, AX_X, ALU.max), "router")
            dve.tensor_tensor(oh, eq, oscore.unsqueeze(2).broadcast_to([P, NCH, R]), ALU.is_equal).then_inc(S["onehot"], 1)
            dve.wait_ge(S["rank_ps"], 1)
            link(dve.tensor_copy(tt, ntok_ps), "router")
            link(dve.tensor_tensor_scan(incl.rearrange("p e c -> p (e c)"), cc("scan0"),
                                        tt.rearrange("p e c -> p (e c)"), 0.0, ALU.mult, ALU.add), "router")
            link(dve.tensor_tensor(off, incl[:, :, NCH - 1:NCH].broadcast_to([P, R, NCH]),
                                   cc("fill").unsqueeze(1).broadcast_to([P, R, NCH]), ALU.is_gt), "router")
            link(dve.tensor_reduce(nblk[:, 0, :], off, AX_X, ALU.add), "router")
            link(dve.tensor_tensor_scan(nblk[:, 1, :], cc("one7"), nblk[:, 0, :], 0.0, ALU.mult, ALU.add), "router")
            link(dve.tensor_tensor(nblk[:, 2, :], nblk[:, 1, :], nblk[:, 0, :], ALU.subtract), "router")
            link(dve.tensor_tensor(off, incl, tt, ALU.subtract), "router")
            link(dve.scalar_tensor_tensor(off, nblk[:, 2, :].unsqueeze(2).broadcast_to([P, R, NCH]), float(P), off,
                                          ALU.mult, ALU.add), "router")
            link(dve.tensor_tensor(eq, rank_ps, off.rearrange("p e c -> p c e"), ALU.add), "router")
            link(dve.tensor_tensor(eq, eq, oh, ALU.mult), "router")
            link(dve.tensor_reduce(slot, eq, AX_X, ALU.add), "router")
            dve.tensor_copy(slot_i[:], slot).then_inc(S["slots"], 1)
            link(dve.tensor_tensor(bcmp, cc("blk")[0:1].unsqueeze(2).broadcast_to([1, NBLK, R - 1]),
                                   nblk[0:1, 1, 0:R - 1].unsqueeze(1).broadcast_to([1, NBLK, R - 1]), ALU.is_ge), "router")
            link(dve.tensor_reduce(bsum, bcmp, AX_X, ALU.add), "router")
            dve.tensor_scalar(expert[:], bsum, 1.0, None, ALU.add).then_inc(S["blocks_known"], 1)

            dve.wait_ge(S["lbT_sb"], 1)
            dve.wait_ge(S["tot_ps"], 1)
            for p in range(3):
                dve.tensor_copy(lbS[:, p, :], lbT).then_inc(S["lb_parts"], 1)
                if p < 2:
                    dve.wait_ge(S["lb_parts"], p + 1)
                    link(dve.tensor_tensor(lbT, lbT, lbS[:, p, :], ALU.subtract), "lb_rest")

            dve.wait_ge(S["wq_hi"], 1)
            dve.scalar_tensor_tensor(wql[:], wraw.rearrange("p w d -> p (w d)"), WS, wqh[:],
                                     ALU.mult, ALU.subtract).then_inc(S["wq_lo"], 1)
            dve.tensor_scalar(wo_sb[:], wo_raw, nw_sb[:, 0:1], None, ALU.mult).then_inc(S["wo_ready"], 1)

            def low_w(i):
                for u in range(2):
                    e = bass.ds(2 * i + u, 1)
                    dve.wait_ge(S["w_hi"], 2 * i + u + 1)
                    dve.scalar_tensor_tensor(w13h[:, e, :, 1, :].rearrange("p o w f -> p (o w) f"), wstage[:, u, :, :], WS,
                                             w13h[:, e, :, 0, :].rearrange("p o w f -> p (o w) f"),
                                             ALU.mult, ALU.subtract).then_inc(S["w_lo"], 1)

            loop(dve, E // 2, low_w)

            dve.wait_ge(S["lb_moved"], 16 * 36)
            dve.wait_ge(S["w_lo"], E)
            dve.wait_ge(S["slots"], 1)
            dve.wait_ge(S["blocks_known"], 1)
            dve.wait_ge(S["xl_ready"], NGRP)
            dve.wait_ge(S["init_out"], 16)

            def gate(i):
                for u in range(2):
                    g = 2 * i + u
                    cols = bass.ds(g * GRP * P, GRP * P)
                    dve.wait_ge(S["qk_tanh"], g + 1)
                    dve.scalar_tensor_tensor(qT[:, cols], tq[:, u, 0, :], 1.0, PS[:, 4 * u, :], ALU.add, ALU.mult
                                             ).then_inc(S["qk_f32"], 1)
                    wait(dve, S["qk_hi"], 2 * g - 2)
                    wait(dve, S["qk_lo"], 2 * g - 2)
                    dve.scalar_tensor_tensor(kT[:, u, :], tq[:, u, 1, :], 1.0, PS[:, 4 * u + 1, :], ALU.add, ALU.mult
                                             ).then_inc(S["qk_f32"], 1)
                    dve.wait_ge(S["k_tanh"], g + 1)
                    dve.wait_ge(S["v_ready"], g + 1)
                    kv = PS[:, 4 * u + 2:4 * u + 4, :].rearrange("p b (c n) -> p b c n", n=2 * D)
                    dve.scalar_tensor_tensor(k2[:, bass.ds(g * GRP, GRP), :].rearrange("p (b c) d -> p b c d", c=2),
                                             tk[:, u].rearrange("p (b c) d -> p b c d", c=2), 1.0, kv[:, :, :, 0:D],
                                             ALU.add, ALU.mult).then_inc(S["k2_ready"], 1)
                    dve.wait_ge(S["qk_f32"], 2 * g + 2)
                    wait(dve, S[f"qk_out{u}"], 16 * 6 * i)
                    for t, src in ((0, qT[:, cols]), (1, kT[:, u, :])):
                        dve.wait_ge(S["qk_hi"], 2 * g + 1 + t)
                        dve.tensor_tensor(qkl[:, u, t, :], src, qkh[:, u, t, :], ALU.subtract).then_inc(S["qk_lo"], 1)

            loop(dve, NGRP // 2, gate)

            for u in range(2):
                dve.wait_ge(S[f"qk_out{u}"], 16 * 6 * (NGRP // 2))
            dve.wait_ge(S["decays"], 3)
            dve.wait_ge(S["qk_lo"], 2 * NGRP)
            link(dve.memset(state[:, :, 0, :], 0.0), "state_zero")

            def finish(i, b, k):
                n = 2 * i + b
                u, c = (b - 1) % 2, chunk(i, b, 1)
                dve.wait_ge(S["pe_i"], n)
                dve.wait_ge(S["dve_s1"], n)
                dve.scalar_tensor_tensor(state[:, u, 0, :], state[:, u, 1, :], dec[:, bass.ds(c * NS + 1, 1)],
                                         um[:, u, 1, :], ALU.mult, ALU.add).then_inc(S["dve_s0"], 1)
                dve.wait_ge(S["pe_av"], n)
                wait(dve, S["dve_o"], n - 1)
                dve.tensor_tensor(o1.rearrange("p (h d) -> p h d", d=HD),
                                  PS[:, 4 + u, 256:384].rearrange("p (h d) -> p h d", d=HD),
                                  elb[:, bass.ds(c, 1), :].rearrange("p o h -> p (o h)").unsqueeze(2).broadcast_to([P, H, HD]),
                                  ALU.mult).then_inc(S["dve_o1"], 1)
                dve.wait_ge(S["dve_o1"], n)
                wait(dve, S["pe_t"], n - 2)
                wait(dve, S["act_ss"], n - 2)
                av = PS[0:SUB, 4 + u, 0:2 * D].rearrange("p (h s e) -> p h s e", s=NS, e=HD)
                for s in range(NS):
                    half = slice(s * SUB, (s + 1) * SUB)
                    last = dve.tensor_tensor(o_sb[half, u, :].rearrange("p (h e) -> p h e", e=HD),
                                             o1[half, :].rearrange("p (h e) -> p h e", e=HD),
                                             av[:, :, s, :], ALU.add)
                last.then_inc(S["dve_o"], 1)

            def attend(i):
                for b in range(2):
                    n, c = 2 * i + b, chunk(i, b)
                    dve.wait_ge(S["pe_u"], n + 1)
                    wait(dve, S["dve_s0"], n - 1)
                    dve.tensor_tensor(um[:, b].rearrange("p s (h e) -> p s h e", e=HD),
                                      PS[:, 6 + b, 0:2 * D].rearrange("p (h s e) -> p s h e", s=NS, e=HD),
                                      cc("hmask").unsqueeze(1).unsqueeze(3).broadcast_to([P, NS, H, HD]),
                                      ALU.mult).then_inc(S["dve_um"], 1)
                    dve.wait_ge(S["dve_um"], n + 1)
                    wait(dve, S["pe_i"], n - 1)
                    dve.scalar_tensor_tensor(state[:, b, 1, :], state[:, b, 0, :], dec[:, bass.ds(c * NS, 1)],
                                             um[:, b, 0, :], ALU.mult, ALU.add).then_inc(S["dve_s1"], 1)
                    dve.wait_ge(S["act_e"], n + 1)
                    dve.wait_ge(S["pe_a"], n + 1)
                    wait(dve, S["pe_av"], n - 1)
                    dve.tensor_tensor(pbuf[:, b, :], ebuf[:, b, :], PS[:, 2:4, :].rearrange("p b n -> p (b n)"),
                                      ALU.mult).then_inc(S["dve_p"], 1)
                    if not (isinstance(n, int) and n == 0):
                        finish(i, b, 1)

            loop(dve, CPB, attend, peel=2)
            finish(CPB, 0, 1)

            dve.wait_ge(S["rms_sd"], 1)
            link(dve.reciprocal(rstd, sdv), "rms")

            def sorted_lo(n, u, turn):
                dve.wait_ge(S[f"xrow_in{u}"], 16 * turn + 16)
                dve.tensor_copy(ids[:, bass.ds(n, 1)], xrow[:, u, D:ROW].bitcast(I32)).then_inc(S["id_copied"], 1)
                dve.wait_ge(S["xs_hi"], n + 1)
                wait(dve, S["f_b"], n - 1)
                dve.tensor_tensor(xsl[:, u, :], PS[:, 6 + u, 0:P], xsh[:, u, :], ALU.subtract).then_inc(S["xs_lo"], 1)

            def hidden(ph, n, u):
                dve.wait_ge(S[ph + "silu"], n + 1)
                dve.wait_ge(S[ph + "b"], n + 1)
                wait(dve, S[ph + "y"], n - 1)
                dve.tensor_tensor(hid[:, u, :], silu[:, u, :], PS[:, 2 + u, :], ALU.mult).then_inc(S[ph + "h"], 1)

            def routed(i):
                for v in range(2):
                    n, u = 2 * i + 1 + v, (1 + v) % 2
                    sorted_lo(n + 1, 1 - u, i + 1)
                    hidden("f_", n, u)

            dve.wait_ge(S["pe_w"], NCH)
            sorted_lo(0, 0, 0)
            sorted_lo(1, 1, 0)
            hidden("f_", 0, 0)
            loop(dve, NBLK // 2 - 1, routed)
            hidden("f_", NBLK - 1, 1)

            def combine(i, u, v):
                n = 2 * i + u
                c = bass.ds(n, 1)

                def flat(a):
                    return a.rearrange("p o d -> p (o d)")

                wait(dve, S["dve_t2"], n - 1)
                dve.scalar_tensor_tensor(t1[:, u, :], flat(attn[:, c, :]), rstd[:, c], flat(x_sb[:, c, :]),
                                         ALU.mult, ALU.add).then_inc(S["dve_t1"], 1)
                dve.wait_ge(S["dve_t1"], n + 1)
                dve.wait_ge(S[f"yt_in{u}"], 16 * i + 16)
                wait(dve, S["dve_out"], n - 1)
                dve.scalar_tensor_tensor(t2[:, u, :], yt[:, u, :], g1[:, c], t1[:, u, :],
                                         ALU.mult, ALU.add).then_inc(S["dve_t2"], 1)
                dve.wait_ge(S["dve_t2"], n + 1)
                dve.wait_ge(S["g_y"], n + 1)
                wait(dve, S[f"stored{u}"], 16 * i)
                dve.scalar_tensor_tensor(osb[:, u, :], PS[:, 4 + u, 0:D], g0[:, c], t2[:, u, :],
                                         ALU.mult, ALU.add).then_inc(S["dve_out"], 1)

            dve.wait_ge(S["f_y"], NBLK)
            dve.wait_ge(S["act_attn"], NCH)
            dve.wait_ge(S["gates"], 2)
            hidden("g_", 0, 0)

            def dense(i):
                for v in range(2):
                    n, u = 2 * i + 1 + v, (1 + v) % 2
                    hidden("g_", n, u)
                    combine(i, v, v)

            loop(dve, NCH // 2 - 1, dense)
            hidden("g_", NCH - 1, 1)
            combine(NCH // 2 - 1, 0, 0)
            combine(NCH // 2 - 1, 1, 1)

        @block.tensor
        def _(pe):
            def mm(out_, lhsT, rhs, start=True, stop=True):
                return pe.matmul(out_, lhsT, rhs, start=start, stop=stop)

            def split_product(out_, a_hi, a_lo, b_hi, b_lo):
                mm(out_, a_hi, b_hi, True, False)
                mm(out_, a_hi, b_lo, False, False)
                return mm(out_, a_lo, b_hi, False, True)

            pe.wait_ge(S["const_in"], 16 * NCONSTDMA)

            for g in range(NGRP):
                u = g % 2
                pe.wait_ge(S["xn_ready"], g + 1)
                wait(pe, S["xh_ready"], g - 1)
                for j in range(GRP):
                    last = pe.transpose(PS[:, u, j * P:(j + 1) * P], rows[:, g * GRP + j, 0:D], cc("ident"))
                last.then_inc(S["xnT_ps"], 1)
                pe.wait_ge(S["xnT_sb"], g + 1)
                for j in range(GRP):
                    last = mm(lg[:, g * GRP + j, 0:E + H], xnT[:, u, j * P:(j + 1) * P], wrf_sb[:])
                last.then_inc(S["logits_ready"], 1)

            pe.wait_ge(S["lf_ready"], 1)
            flat = lf[:, 0:NCH * H]
            mm(PS[:, 5, :], cc("cum"), flat)
            mm(PS[:, 6, :], cc("suffix"), flat).then_inc(S["cum_ps"], 1)
            pe.wait_ge(S["xh_ready"], NGRP)
            for c in range(NCH):
                k, col = c // 8, (c % 8) * P
                last = mm(PS[32 * k:32 * k + 32, col // 512, col % 512:col % 512 + P],
                          lf[:, c * H:c * H + 32], cc("cum"))
            last.then_inc(S["lbT_ps"], 1)
            pe.wait_ge(S["lbT_sb"], 1)
            pe.wait_ge(S["router_in"], 1)
            for k in range(4):
                rows_k = slice(32 * k, 32 * k + H)
                last = mm(PS[:, k, 0:NCH * NS // 4], cc("expand")[rows_k],
                          lbT[rows_k, :].rearrange("p (n i) -> p n i", i=SUB)[:, :, SUB - 1])
            last.then_inc(S["tot_ps"], 1)
            pe.wait_ge(S["onehot"], 1)
            flat = oh.rearrange("p c e -> p (c e)")
            mm(PS[:, 4, 0:NCH * R], cc("rank"), flat)
            mm(PS[:, 4, NCH * R:2 * NCH * R], cc("ones"), flat).then_inc(S["rank_ps"], 1)

            pe.wait_ge(S["decays"], 3)
            pe.wait_ge(S["slots"], 1)
            pe.wait_ge(S["wq_lo"], 1)
            pe.wait_ge(S["xl_ready"], NGRP)

            def project(i):
                for u in range(2):
                    g = 2 * i + u
                    cols = bass.ds(g * GRP * P, GRP * P)
                    wait(pe, S["qk_f32"], 2 * g - 2)
                    for t in range(2):
                        w = slice(t * D, (t + 1) * D)
                        last = split_product(PS[:, 4 * u + t, :], wqh[:, w], wql[:, w], xh[:, cols], xl[:, cols])
                    last.then_inc(S["q_ps"], 1)
                    wait(pe, S["k2_ready"], g - 1)
                    wait(pe, S["v_ready"], g - 1)
                    for j in range(GRP):
                        tok = bass.ds(g * GRP * P + j * P, P)
                        last = split_product(PS[:, 4 * u + 2 + j // 2, (j % 2) * 2 * D:(j % 2 + 1) * 2 * D],
                                             xh[:, tok], xl[:, tok], wqh[:, D:3 * D], wql[:, D:3 * D])
                    last.then_inc(S["kv_ps"], 1)

            loop(pe, NGRP // 2, project)

            pe.wait_ge(S["qk_f32"], 2 * NGRP)
            pe.wait_ge(S["k2_ready"], NGRP)
            pe.wait_ge(S["v_ready"], NGRP)
            pe.wait_ge(S["dstat_in"], 16 * 5)
            pe.wait_ge(S["wo_ready"], 1)
            pe.wait_ge(S["state_zero"], 1)

            def attend(i):
                for b in range(2):
                    n = 2 * i + b
                    known = isinstance(n, int)

                    def has(k):
                        return not known or 0 <= n - k < NCH

                    u = 1 - b
                    if has(2):
                        pe.wait_ge(S["dve_o"], n - 1)
                        wait(pe, S["act_ot"], n - 3)
                        pe.transpose(PS[:, 4 + b, 384:512], o_sb[:, b, :], cc("ident")).then_inc(S["pe_t"], 1)
                    if has(0):
                        pe.wait_ge(S["pool_kd"], n + 1)
                        pe.wait_ge(S["pool_v2"], n + 1)
                        wait(pe, S["dve_um"], n - 1)
                        wait(pe, S["act_attn"], n - 3)
                        mm(PS[:, 6 + b, 0:2 * D], kd[:, b, :], v2[:, b, :]).then_inc(S["pe_u"], 1)
                        pe.wait_ge(S[f"dr_in{b}"], 16 * i + 16)
                        wait(pe, S["act_e"], n)
                        for half in range(2):
                            last = mm(PS[:, half, :], dL[:, bass.ds(chunk(i, b), 1), :].rearrange("p o t -> p (o t)"),
                                      dR[:, b, half * 512:(half + 1) * 512])
                        last.then_inc(S["pe_d"], 1)
                        pe.wait_ge(S[f"st_in{b}"], 32 * i + 32)
                        wait(pe, S["dve_p"], n)
                        for h in range(H):
                            for s in range(NS):
                                tok = slice(s * SUB, (s + 1) * SUB)
                                last = mm(PS[tok, 2 + h // 8, (h % 8) * SUB:(h % 8 + 1) * SUB],
                                          k_st[:, b, h, tok], q_st[:, b, h, tok])
                        last.then_inc(S["pe_a"], 1)
                    if has(1):
                        pe.wait_ge(S["dve_s1"], n)
                        wait(pe, S["dve_s0"], n - 2)
                        wait(pe, S["dve_o"], n - 2)
                        wait(pe, S["act_ot"], n - 2)
                        pe.wait_ge(S[f"q_in{u}"], 16 * (i + (b - 1) // 2) + 16)
                        for s in range(NS):
                            tok = slice(s * SUB, (s + 1) * SUB)
                            last = mm(PS[tok, 4 + u, 256:384], q_now[:, u, tok], state[:, u, s, :])
                        last.then_inc(S["pe_i"], 1)
                        pe.wait_ge(S["dve_p"], n)
                        for h in range(H):
                            last = mm(PS[0:SUB, 4 + u, h * NS * HD:(h + 1) * NS * HD],
                                      pbuf[:, u, h * SUB:(h + 1) * SUB], v2[:, u, h * NS * HD:(h + 1) * NS * HD])
                        last.then_inc(S["pe_av"], 1)
                    if has(2):
                        pe.wait_ge(S["act_ot"], n - 1)
                        pe.wait_ge(S["dve_um"], min(n + 1, NCH) if known else n + 1)
                        mm(PS[:, 6 + b, 256:384], oT[:, b, :], wo_sb[:]).then_inc(S["pe_w"], 1)

            loop(pe, CPB, attend, peel=2)
            attend(CPB)

            def turn_rows(n, u, turn):
                pe.wait_ge(S[f"xrow_in{u}"], 16 * turn + 16)
                wait(pe, S["xs_lo"], n - 1)
                pe.transpose(PS[:, 6 + u, 0:P], xrow[:, u, 0:D], cc("ident")).then_inc(S["xs_ps"], 1)

            def up(ph, n, u, e, hi, lo):
                wait(pe, S[ph + "silu"], n - 1)
                wait(pe, S[ph + "h"], n - 1)
                for w in range(2):
                    for f in range(FB):
                        cols = slice(f * P, (f + 1) * P)
                        wt = [w13h[:, bass.ds(e, 1), w, part, cols].rearrange("p o f -> p (o f)") for part in range(2)]
                        last = split_product(PS[:, 2 * w + u, cols], wt[0], wt[1], hi, lo)
                    last.then_inc(S[ph + "ab"[w]], 1)

            def down(ph, n, u, e, y_free):
                pe.wait_ge(S[ph + "h"], n + 1)
                wait(pe, S[y_free], n - 1)
                for f in range(FB):
                    last = mm(PS[:, 4 + u, 0:D], hid[:, u, f * P:(f + 1) * P],
                              w2_sb[:, bass.ds(e, 1), f, :].rearrange("p o d -> p (o d)"),
                              f == 0, f == FB - 1)
                last.then_inc(S[ph + "y"], 1)

            def expert_of(n):
                return pe.value_load(expert[0:1, bass.ds(n, 1)], min_val=1, max_val=E - 1)

            def up_routed(n, u):
                pe.wait_ge(S["xs_hi"], n + 1)
                pe.wait_ge(S["xs_lo"], n + 1)
                up("f_", n, u, expert_of(n), xsh[:, u, :], xsl[:, u, :])

            pe.wait_ge(S["act_attn"], NCH)
            pe.wait_ge(S["dve_p"], NCH)
            pe.wait_ge(S["w_lo"], E)
            pe.wait_ge(S["w2_in"], 16)
            turn_rows(0, 0, 0)
            turn_rows(1, 1, 0)
            up_routed(0, 0)

            def routed(i):
                for v in range(2):
                    n, u = 2 * i + 1 + v, (1 + v) % 2
                    turn_rows(n + 1, 1 - u, i + 1)
                    up_routed(n, u)
                    down("f_", n - 1, 1 - u, expert_of(n - 1), "y_sb")

            loop(pe, NBLK // 2 - 1, routed)
            up_routed(NBLK - 1, 1)
            down("f_", NBLK - 2, 0, expert_of(NBLK - 2), "y_sb")
            down("f_", NBLK - 1, 1, expert_of(NBLK - 1), "y_sb")

            pe.wait_ge(S["f_h"], NBLK)
            pe.wait_ge(S["y_sb"], NBLK)

            def up_dense(n, u):
                tok = bass.ds(n * P, P)
                up("g_", n, u, 0, xh[:, tok], xl[:, tok])

            up_dense(0, 0)

            def dense(i):
                for v in range(2):
                    n, u = 2 * i + 1 + v, (1 + v) % 2
                    up_dense(n, u)
                    down("g_", n - 1, 1 - u, 0, "dve_out")

            loop(pe, NCH // 2 - 1, dense)
            up_dense(NCH - 1, 1)
            down("g_", NCH - 2, 0, 0, "dve_out")
            down("g_", NCH - 1, 1, 0, "dve_out")


def kernel(L0_attn_x, L0_attn_Wq, L0_attn_Wk, L0_attn_Wv, L0_attn_Wo, L0_attn_Wf, L0_attn_delta,
           L0_attn_norm_weight, L0_ffn_Wr, L0_ffn_W1, L0_ffn_W2, L0_ffn_W3):
    import concourse.bacc as bacc
    from concourse.bass_utils import run_bass_kernel_spmd

    dleft, dright = decay_constants()
    arrays = {
        "x": np.ascontiguousarray(L0_attn_x).reshape(TOK, D),
        "wqkv": np.ascontiguousarray(np.stack([np.asarray(w).T for w in (L0_attn_Wq, L0_attn_Wk, L0_attn_Wv)], 1)),
        "wo": np.ascontiguousarray(np.asarray(L0_attn_Wo).T),
        "wrf": np.ascontiguousarray(np.concatenate([np.asarray(L0_ffn_Wr), np.asarray(L0_attn_Wf)], 0).T),
        "delta": np.ascontiguousarray(L0_attn_delta),
        "nw": np.ascontiguousarray(L0_attn_norm_weight).reshape(D, 1),
        "w13": np.ascontiguousarray(np.stack([np.asarray(L0_ffn_W1), np.asarray(L0_ffn_W3)], 1).transpose(3, 0, 1, 2)),
        "w2": np.ascontiguousarray(np.asarray(L0_ffn_W2).reshape(E, D, FB, P).transpose(3, 0, 2, 1)),
        "const": constants(),
        "dleft": dleft,
        "dright": dright,
    }
    nc = bacc.Bacc("TRN2", target_bir_lowering=False, num_devices=1)
    args = [nc.dram_tensor(n, a.shape, mybir.dt.from_np(a.dtype), kind="ExternalInput").ap() for n, a in arrays.items()]
    args.append(nc.dram_tensor("out", (TOK, D), F32, kind="ExternalOutput").ap())
    for n, shape, dt in (("qk_scr", (2, 3, HD, H, TOK), F16), ("lb_scr", (NCH, 3, NS, H, SUB), BF16),
                         ("xsort", (NBLK * P, ROW), F32), ("ytok", (TOK + NBLK * P, D), F32)):
        args.append(nc.dram_tensor(n, shape, dt, kind="Internal").ap())
    build(nc, *args)
    r = run_bass_kernel_spmd(nc, [arrays], core_ids=[0])
    return np.asarray(r.results[0]["out"]).reshape(BATCH, SEQ, D)
```

```python
from contextlib import ExitStack

import numpy as np
import concourse.bass as bass
from concourse import mybir

F32 = mybir.dt.float32
F16 = mybir.dt.float16
BF16 = mybir.dt.bfloat16
I32 = mybir.dt.int32
ALU = mybir.AluOpType
ACT = mybir.ActivationFunctionType
AX_X = mybir.AxisListType.X

P = 128
BATCH, SEQ, D = 2, 2048, 128
TOK = BATCH * SEQ
NCH = TOK // P
CPB = NCH // BATCH
H, HD = 16, 8
SUB = 64
NS = P // SUB
E, FF = 8, 512
FB = FF // P
R = E - 1
GRP = 4
NGRP = NCH // GRP
NBLK = NCH + R - 1
ROW = D + 1
LN_EPS, RMS_EPS = 1e-5, 1e-6
WS = 64.0
QS = 2.0 * WS
OS = QS * QS * WS
BIG = -1.0e30
DROWS = 3 * H + 3 * NS + SUB
NLB, NSEL = 3 * H, 3 * NS

COLS = {}
_at = 0
for _name, _n in [("ident", P), ("hmask", H), ("smask", NS),
                  ("rank", P), ("ones", P), ("cum", P), ("suffix", P), ("expand", P),
                  ("scan0", R * NCH), ("one7", R), ("order", R), ("fill", NCH), ("blk", NBLK)]:
    COLS[_name] = (_at, _at + _n)
    _at += _n
NCONST = _at
NKEPT = COLS["smask"][1]


def constants():
    k = np.arange(P)[:, None]
    m = np.arange(P)[None, :]
    same = (k // SUB) == (m // SUB)
    c = np.zeros((P, NCONST), np.float32)

    def put(name, v):
        a, b = COLS[name]
        c[:, a:b] = v

    put("rank", k < m)
    put("ones", 1)
    put("cum", (k <= m) & same)
    put("suffix", (k > m) & same)
    put("ident", k == m)
    put("expand", (k % 32 == m // HD))
    put("scan0", (np.arange(R * NCH) % NCH != 0)[None])
    put("one7", 1)
    put("order", (R - np.arange(R))[None])
    put("fill", (P * np.arange(NCH))[None])
    put("blk", np.arange(NBLK)[None])
    put("hmask", k // HD == np.arange(H)[None])
    put("smask", k // SUB == np.arange(NS)[None])
    return c


def decay_constants():
    j = np.arange(P)
    left = np.zeros((NSEL + SUB, P), np.float32)
    for p in range(3):
        for s in range(NS):
            left[p * NS + s] = (j // SUB == s)
    left[NSEL:] = (np.arange(SUB)[:, None] == (j % SUB)[None])
    right = np.zeros((DROWS, H, SUB), np.float32)
    for p in range(3):
        for h in range(H):
            right[p * H + h, h] = -1
    right[NLB + NSEL:] = np.where(np.arange(SUB)[None, None, :] < np.arange(SUB)[:, None, None], BIG, 0)


    def bits(a):
        return (np.ascontiguousarray(a).view(np.uint32) >> 16).astype(np.uint16)

    return bits(left), bits(right.reshape(DROWS, H * SUB))



def build(nc, x, wqkv, wo, wrf, delta, nw, w13, w2, const, dleft, dright, out,
          qk_scr, lb_scr, xsort, ytok):
    dleft, dright = dleft.bitcast(BF16), dright.bitcast(BF16)
    with ExitStack() as ctx:
        def sb(name, shape, dt=F32):
            return ctx.enter_context(nc.sbuf_tensor(name, shape, dt))

        def sem(name):
            return ctx.enter_context(nc.semaphore(name))

        def wait(eng, s, value):
            if isinstance(value, int) and value <= 0:
                return
            eng.wait_ge(s, value)

        def at(eng, value):
            return value if isinstance(value, int) else eng.snap(value)

        def loop(eng, count, body, peel=1):
            for i in range(peel):
                body(i)
            if peel < count:
                with eng.Fori(peel, count) as i:
                    body(i)

        class Region:

            def __init__(self, name, kib):
                self.tensor, self.at, self.size = sb(name, [P, kib * 256]), 0, kib * 256

            def take(self, shape, dt=F32):
                per = 1 if dt in (F32, I32) else 2
                n = int(np.prod(shape[1:]))
                words = -(-n // per)
                a = self.at
                self.at += words
                assert self.at <= self.size, (self.at, self.size)
                v = self.tensor[0:shape[0], a:a + words]
                if dt != F32:
                    v = v.bitcast(dt)
                names = "abcd"[:len(shape) - 1]
                if len(shape) > 2:
                    v = v.rearrange(f"p ({' '.join(names)}) -> p {' '.join(names)}",
                                    **{k: m for k, m in zip(names[1:], shape[2:])})
                return v

            def again(self, at=0):
                self.at = at

        PS = ctx.enter_context(nc.psum_tensor("PS", [P, 8, 512], F32))
        kept_cst = sb("kept_cst", [P, NKEPT])
        w2_first = sb("w2_first", [P, FB, D])

        x_sb = sb("x_sb", [P, NCH, D])
        rows = sb("rows", [P, NCH, ROW])
        attn = rows[:, :, 0:D]
        xh = sb("xh", [P, TOK], F16)
        xl = sb("xl", [P, TOK], F16)
        w13h = sb("w13h", [P, E, 2, 2, FF], F16)
        elb = sb("elb", [P, NCH, H])
        sdec = sb("sdec", [P, NCH, H])
        dec = sb("dec", [P, NCH * NS])
        small = sb("small", [P, 12, NCH])
        mean_var = sb("mean_var", [P, 2, GRP, 2])
        stats = sb("stats", [P, 2, GRP, 6])
        g0, g1, ssq, sdv, rstd = (small[:, k, :] for k in range(5))
        rmax, rsum, ptop, den, den2, oscore, slot = (small[:, k, :] for k in range(5, 12))
        slot_i = sb("slot_i", [P, NCH], I32)
        expert = sb("expert", [1, NBLK], I32)
        ids = sb("ids", [P, NBLK], I32)
        eps = sb("eps", [P, 3])
        eps_ln, eps_rms, one = eps[:, 0:1], eps[:, 1:2], eps[:, 2:3]
        wrf_sb = sb("wrf_sb", [P, E + H])
        delta_sb = sb("delta_sb", [P, H])
        nw_sb = sb("nw_sb", [P, 1])
        wo_sb = sb("wo_sb", [P, D])
        wqh = sb("wqh", [P, 3 * D], F16)
        wql = sb("wql", [P, 3 * D], F16)

        Z = Region("Z", 48)
        early_cst = Z.take([P, NCONST - NKEPT])
        lf = Z.take([P, (NCH + 1) * H])
        wraw = Z.take([P, 3, D])
        wo_raw = Z.take([P, D])
        rl = Z.take([P, NCH, E])
        rexp = Z.take([P, NCH, E])
        eq = Z.take([P, NCH, R])
        oh = Z.take([P, NCH, R])
        tt = Z.take([P, R, NCH])
        incl = Z.take([P, R, NCH])
        off = Z.take([P, R, NCH])
        bcmp = Z.take([1, NBLK, R - 1])
        bsum = Z.take([1, NBLK])
        nblk = Z.take([P, 3, R])
        zf = Z.take([P, NCH, H])
        zm = Z.take([P, NCH, H])
        ze = Z.take([P, NCH, H])
        lbT = Z.take([P, 8 * P])
        lbS = Z.take([P, 3, 8 * P], BF16)
        wstage = Z.take([P, 2, 2, FF])
        Z.again()
        qT = Z.take([P, TOK])
        k2 = Z.take([P, NCH, D])
        v_sb = Z.take([P, NCH, D])
        Z.again()
        w2_sb = Z.take([P, E, FB, D])

        def cc(name):
            a, b = COLS[name]
            return kept_cst[:, a:b] if b <= NKEPT else early_cst[:, a - NKEPT:b - NKEPT]

        C = Region("C", 44)
        xnT = C.take([P, 2, GRP * P])
        zero = C.take([P, NBLK, ROW])
        C.again()
        tq = C.take([P, 2, 2, GRP * P])
        tk = C.take([P, 2, GRP, P])
        kT = C.take([P, 2, GRP * P])
        qkh = C.take([P, 2, 2, GRP * P], F16)
        qkl = C.take([P, 2, 2, GRP * P], F16)
        C.again()
        q_st = C.take([3 * HD, 2, H, P], F16)
        k_st = C.take([3 * HD, 2, H, P], F16)
        ebuf = C.take([P, 2, H * SUB // 2])
        pbuf = C.take([P, 2, H * SUB])
        kd = C.take([P, 2, D])
        v2 = C.take([P, 2, H * NS * HD])
        um = C.take([P, 2, NS, D])
        state = C.take([P, 2, NS, D])
        q_now = C.take([P, 2, P])
        o1 = C.take([P, D])
        o_sb = C.take([P, 2, D])
        junk = C.take([P, 2, D])
        oT = C.take([P, 2, D])
        hid0 = C.take([P, 2, FF])
        C.again()
        xrow = C.take([P, 2, ROW])
        xsh = C.take([P, 2, P], F16)
        xsl = C.take([P, 2, P], F16)
        silu = C.take([P, 2, FF])
        hid = C.take([P, 2, FF])
        ysb = C.take([P, 2, D])
        yt = C.take([P, NCH, D])
        dL = sb("dL", [DROWS, NCH, P], BF16)
        dR = sb("dR", [DROWS, 2, H * SUB], BF16)

        class Sems(dict):
            def __missing__(self, name):
                self[name] = sem(name)
                return self[name]

        S = Sems()
        NCONSTDMA = 8

        lg = PS[:, 2:4, :].rearrange("p b (c n) -> p (b c) n", n=2 * 512 // NCH)
        rank_ps = PS[:, 4, 0:NCH * R].rearrange("p (c e) -> p c e", e=R)
        ntok_ps = PS[:, 4, NCH * R:2 * NCH * R].rearrange("p (c e) -> p e c", e=R)

        def chunk(i, b, k=0):
            return ((b - k) % 2) * CPB + i + (b - k) // 2

        NQ = 4

        def quarter(q):
            return slice(q * NCH // NQ, (q + 1) * NCH // NQ)

        block = ctx.enter_context(nc.Block())

        @block.sync
        def _(sp):
            def load_x(i):
                for u in range(2):
                    g = 2 * i + u
                    gs = bass.ds(at(sp, g * GRP), GRP)
                    wait(sp, S[f"x_in{u}"], 16 * i)
                    sp.dma_start(x_sb[:, gs, :], x.rearrange("(c p) d -> p c d", p=P)[:, gs, :]
                                 ).then_inc(S[f"x_in{u}"], 16)

            loop(sp, NGRP // 2, load_x)

            def load_w(i):
                for u in range(2):
                    e = at(sp, 2 * i + u)
                    wait(sp, S["w_lo"], 2 * i + u - 1)
                    sp.dma_start(wstage[:, u, :, :], w13[:, bass.ds(e, 1)].rearrange("p o w f -> p (o w) f")
                                 ).then_inc(S[f"stage_in{u}"], 16)

            loop(sp, E // 2, load_w)

            sp.wait_ge(S["lb_parts"], 3)
            for k in range(4):
                for p in range(3):
                    src = lbS[32 * k:32 * k + H, p, :]
                    sp.dma_start(dL[p * H:(p + 1) * H, 8 * k:8 * k + 8, :], src.rearrange("p (c t) -> p c t", t=P)
                                 ).then_inc(S["lb_moved"], 16)
                    for s in range(NS):
                        sp.dma_start(lb_scr[8 * k:8 * k + 8, p, s].rearrange("c h i -> h c i"),
                                     src.rearrange("p (c s i) -> p c s i", s=NS, i=SUB)[:, :, s, :]
                                     ).then_inc(S["lb_moved"], 16)

            def store_parts(i):
                for u in range(2):
                    g = 2 * i + u
                    cols = bass.ds(at(sp, g * GRP * P), GRP * P)
                    sp.wait_ge(S["qk_hi"], 2 * g + 2)
                    sp.wait_ge(S["qk_lo"], 2 * g + 2)
                    for t in range(2):
                        for p, src in enumerate([qkh, qkl, qkh] if t == 0 else [qkh, qkh, qkl]):
                            sp.dma_start(
                                qk_scr[t, p].rearrange("d h t -> h d t")[:, :, cols],
                                src[:, u, t, :]).then_inc(S[f"qk_out{u}"], 16)

            loop(sp, NGRP // 2, store_parts)

            sp.wait_ge(S["lb_moved"], 16 * 36)
            for u in range(2):
                sp.wait_ge(S[f"qk_out{u}"], 16 * 6 * (NGRP // 2))

            def load_stacks(i):
                for b in range(2):
                    n, c = 2 * i + b, chunk(i, b)
                    tok, cs = bass.ds(at(sp, c * P), P), bass.ds(at(sp, c), 1)
                    used, products_used = at(sp, n - 1), at(sp, 2 * n - 2)
                    dr_src = lb_scr[cs].rearrange("o p s h i -> (o p s) (h i)")
                    wait(sp, S["pe_a"], products_used)
                    wait(sp, S["pe_d"], products_used)
                    for t, dst in ((0, q_st), (1, k_st)):
                        sp.dma_start(dst[:, b, :, :],
                                     qk_scr[t].rearrange("p d h t -> (p d) h t")[:, :, tok]
                                     ).then_inc(S[f"st_in{b}"], 16)
                    sp.dma_start(dR[NLB:NLB + NSEL, b, :], dr_src).then_inc(S[f"dr_in{b}"], 16)
                    wait(sp, S["pe_i"], used)
                    sp.dma_start(q_now[:, b, :], qT[:, tok]).then_inc(S[f"q_in{b}"], 16)

            loop(sp, CPB, load_stacks)

            for b in range(2):
                sp.wait_ge(S[f"q_in{b}"], 16 * CPB)
            sp.dma_start(w2_sb[:, 1:E], w2[:, 1:E]).then_inc(S["w2_in"], 16)
            for b in range(2):
                sp.wait_ge(S[f"scattered{b}"], 16 * CPB)
            sp.wait_ge(S["pe_w"], NCH)
            sp.wait_ge(S["act_ss"], NCH)
            sp.wait_ge(S["g_y"], NCH)

            def load_rows(i):
                for u in range(2):
                    n = 2 * i + u
                    tok = bass.ds(at(sp, n * P), P)
                    wait(sp, S["xs_ps"], n - 1)
                    wait(sp, S["id_copied"], n - 1)
                    sp.dma_start(xrow[:, u, :], xsort[tok, :]).then_inc(S[f"xrow_in{u}"], 16)

            loop(sp, NBLK // 2, load_rows)

            for u in range(2):
                sp.wait_ge(S[f"y_out{u}"], 16 * (NBLK // 2))
            token_rows = [t[0:TOK].rearrange("(c p) d -> p c d", p=P) for t in (ytok, out)]
            for q in range(NQ):
                sp.dma_start(yt[:, quarter(q)], token_rows[0][:, quarter(q)]).then_inc(S[f"yt_in{q}"], 16)
            for q in range(NQ):
                sp.wait_ge(S["dve_out"], (q + 1) * NCH // NQ)
                sp.dma_start(token_rows[1][:, quarter(q)], yt[:, quarter(q)]).then_inc(S["stored"], 16)
            sp.wait_ge(S["stored"], 16 * NQ)

        @block.gpsimd
        def _(pool):
            pool.memset(zero, 0.0).then_inc(S["pool_init"], 1)
            pool.iota(rows[:, :, D].bitcast(I32), pattern=[[P, NCH]], base=0, channel_multiplier=1
                      ).then_inc(S["pool_init"], 1)
            pool.wait_ge(S["pool_init"], 2)
            pool.iota(zero[:, :, D].bitcast(I32), pattern=[[1, NBLK]], base=TOK, channel_multiplier=NBLK
                      ).then_inc(S["pool_init"], 1)
            pool.wait_ge(S["pool_init"], 3)
            pool.dma_start(xsort.rearrange("(p n) r -> p n r", n=NBLK), zero).then_inc(S["init_out"], 16)

            def low(i):
                for u in range(2):
                    g = 2 * i + u
                    cols = bass.ds(g * GRP * P, GRP * P)
                    pool.wait_ge(S["xnT_sb"], g + 1)
                    pool.wait_ge(S["xh_ready"], g + 1)
                    pool.tensor_tensor(xl[:, cols], xnT[:, u, :], xh[:, cols], ALU.subtract).then_inc(S["xl_ready"], 1)

            loop(pool, NGRP // 2, low)

            pool.wait_ge(S["const_in"], 16 * NCONSTDMA)
            pool.wait_ge(S["init_out"], 16)
            pool.wait_ge(S["slots"], 1)
            for n in range(NCH):
                b, c = n % 2, chunk(n // 2, n % 2)
                wait(pool, S[f"scattered{b}"], 16 * (n // 2))
                pool.indirect_dma_start(xsort, bass.IndirectOffsetOnAxis(ap=slot_i[:, c:c + 1], axis=0),
                                        rows[:, c, :], None).then_inc(S[f"scattered{b}"], 16)
                if n == 0:
                    pool.wait_ge(S["decays"], 3)
                    pool.wait_ge(S["k2_ready"], NGRP)
                    pool.wait_ge(S["v_ready"], NGRP)
                    pool.wait_ge(S["qk_lo"], 2 * NGRP)
                    for u in range(2):
                        pool.wait_ge(S[f"qk_out{u}"], 16 * 6 * (NGRP // 2))
                wait(pool, S["pe_u"], n - 1)
                pool.tensor_tensor(kd[:, b, :].rearrange("p (h d) -> p h d", d=HD),
                                   k2[:, c, :].rearrange("p (h d) -> p h d", d=HD),
                                   sdec[:, c, :].unsqueeze(2).broadcast_to([P, H, HD]),
                                   ALU.mult).then_inc(S["pool_kd"], 1)
                wait(pool, S["pe_av"], n - 1)
                pool.tensor_tensor(v2[:, b, :].rearrange("p (h s e) -> p h s e", s=NS, e=HD),
                                   v_sb[:, c, :].rearrange("p (h e) -> p h e", e=HD).unsqueeze(2)
                                   .broadcast_to([P, H, NS, HD]),
                                   cc("smask").unsqueeze(1).unsqueeze(3).broadcast_to([P, H, NS, HD]),
                                   ALU.mult).then_inc(S["pool_v2"], 1)

            pool.wait_ge(S["rms"], 1)
            for n in range(NBLK):
                pool.wait_ge(S["y_sb"], n + 1)
                pool.wait_ge(S["id_copied"], n + 1)
                pool.indirect_dma_start(ytok, bass.IndirectOffsetOnAxis(ap=ids[:, n:n + 1], axis=0),
                                        ysb[:, n % 2, :], None).then_inc(S[f"y_out{n % 2}"], 16)
                if n < NCH:
                    pool.tensor_scalar(attn[:, n, :], attn[:, n, :], rstd[:, n:n + 1], None, ALU.mult
                                       ).then_inc(S["pool_attn"], 1)
                    pool.wait_ge(S["pool_attn"], n + 1)
                    pool.tensor_tensor(x_sb[:, n, :], x_sb[:, n, :], attn[:, n, :], ALU.add).then_inc(S["x_done"], 1)

        @block.scalar
        def _(act):
            for dst, src in ((kept_cst[:], const[:, 0:NKEPT]), (early_cst, const[:, NKEPT:NCONST]),
                             (w2_first[:], w2[:, 0]), (wrf_sb[:], wrf), (delta_sb[:], delta.partition_broadcast(P)),
                             (nw_sb[:], nw), (wo_raw, wo), (wraw, wqkv)):
                act.dma_start(dst, src).then_inc(S["const_in"], 16)
            for b in range(2):
                act.dma_start(dR[0:NLB, b, :], dright[0:NLB, :]).then_inc(S["dstat_in"], 16)
                act.dma_start(dR[NLB + NSEL:DROWS, b, :], dright[NLB + NSEL:DROWS, :]).then_inc(S["dstat_in"], 16)
            act.dma_start(dL[NLB:DROWS, :, :], dleft.unsqueeze(1).broadcast_to([NSEL + SUB, NCH, P])
                          ).then_inc(S["dstat_in"], 16)

            act.wait_ge(S["eps_set"], 3)

            def transposed(i):
                for u in range(2):
                    g = 2 * i + u
                    gs = bass.ds(g * GRP, GRP)
                    act.wait_ge(S["ln_aggr"], g + 1)
                    act.activation(sdv[:, gs], mean_var[:, u, :, 1], ACT.Sqrt, bias=eps_ln).then_inc(S["ln_sd"], 1)
                    act.wait_ge(S["xnT_ps"], g + 1)
                    wait(act, S["logits_ready"], g - 1)
                    wait(act, S["xl_ready"], g - 1)
                    act.activation(xnT[:, u, :], PS[:, u, :], ACT.Copy).then_inc(S["xnT_sb"], 1)
                    act.activation(xh[:, bass.ds(g * GRP * P, GRP * P)], PS[:, u, :], ACT.Copy).then_inc(S["xh_ready"], 1)

            loop(act, NGRP // 2, transposed)

            act.wait_ge(S["const_in"], 16 * NCONSTDMA)
            act.activation(wqh[:], wraw.rearrange("p w d -> p (w d)"), ACT.Copy, scale=WS).then_inc(S["wq_hi"], 1)

            act.wait_ge(S["forget_abs"], 1)
            act.activation(ze, ze, ACT.Exp).then_inc(S["forget_exp"], 1)
            act.wait_ge(S["forget_exp"], 1)
            act.activation(ze, ze, ACT.Ln, bias=one).then_inc(S["forget_ln"], 1)
            act.wait_ge(S["router_in"], 1)
            act.activation(rexp, rl, ACT.Exp).then_inc(S["router_exp"], 1)
            act.wait_ge(S["cum_ps"], 1)
            act.activation(elb[:].rearrange("p c h -> p (c h)"), PS[:, 5, :], ACT.Exp).then_inc(S["decays"], 1)
            act.activation(sdec[:].rearrange("p c h -> p (c h)"), PS[:, 6, :], ACT.Exp).then_inc(S["decays"], 1)
            act.wait_ge(S["lbT_ps"], 1)
            act.activation(lbT, PS[:, 0:2, :].rearrange("p b n -> p (b n)"), ACT.Copy).then_inc(S["lbT_sb"], 1)
            act.wait_ge(S["tot_ps"], 1)
            act.activation(dec[:].rearrange("p (k n) -> p k n", k=4), PS[:, 0:4, 0:NCH * NS // 4], ACT.Exp
                           ).then_inc(S["decays"], 1)

            def high_w(i):
                for u in range(2):
                    act.wait_ge(S[f"stage_in{u}"], 16 * i + 16)
                    act.activation(w13h[:, bass.ds(2 * i + u, 1), :, 0, :].rearrange("p o w f -> p (o w) f"),
                                   wstage[:, u, :, :], ACT.Copy, scale=WS).then_inc(S["w_hi"], 1)

            loop(act, E // 2, high_w)

            def project(i):
                for u in range(2):
                    g = 2 * i + u
                    act.wait_ge(S["q_ps"], g + 1)
                    wait(act, S["qk_f32"], 2 * g - 2)
                    for t in range(2):
                        last = act.activation(tq[:, u, t, :], PS[:, 4 * u + t, :], ACT.Tanh, scale=0.5 / WS)
                    last.then_inc(S["qk_tanh"], 1)
                    act.wait_ge(S["kv_ps"], g + 1)
                    wait(act, S["k2_ready"], g - 1)
                    kv = PS[:, 4 * u + 2:4 * u + 4, :].rearrange("p b (c n) -> p b c n", n=2 * D)
                    act.activation(tk[:, u].rearrange("p (b c) d -> p b c d", c=2), kv[:, :, :, 0:D], ACT.Tanh,
                                   scale=0.5 / WS).then_inc(S["k_tanh"], 1)
                    act.activation(v_sb[:, bass.ds(g * GRP, GRP), :].rearrange("p (b c) d -> p b c d", c=2),
                                   kv[:, :, :, D:2 * D], ACT.Copy).then_inc(S["v_ready"], 1)
                    act.wait_ge(S["qk_f32"], 2 * g + 2)
                    wait(act, S[f"qk_out{u}"], 16 * 6 * i)
                    wait(act, S["qk_lo"], 2 * g - 2)
                    act.activation(qkh[:, u, 0, :], qT[:, bass.ds(g * GRP * P, GRP * P)], ACT.Copy).then_inc(S["qk_hi"], 1)
                    act.activation(qkh[:, u, 1, :], kT[:, u, :], ACT.Copy).then_inc(S["qk_hi"], 1)

            act.wait_ge(S["lb_moved"], 16 * 36)
            act.wait_ge(S["w_lo"], E)
            act.wait_ge(S["slots"], 1)
            act.wait_ge(S["blocks_known"], 1)
            act.wait_ge(S["xl_ready"], NGRP)
            act.wait_ge(S["init_out"], 16)
            loop(act, NGRP // 2, project)

            def attend(i):
                for b in range(2):
                    n = 2 * i + b
                    known = isinstance(n, int)

                    def has(k):
                        return not known or 0 <= n - k < NCH

                    def decays(half):
                        act.wait_ge(S["pe_d"], 2 * n + half + 1)
                        wait(act, S["dve_p"], 2 * n + half - 1)
                        act.activation(ebuf[:, half, :], PS[:, 0, :], ACT.Exp).then_inc(S["act_e"], 1)

                    if has(0):
                        decays(0)
                    if has(3):
                        u = (b - 3) % 2
                        act.wait_ge(S["pe_w"], n - 2)
                        act.wait_ge(S[f"scattered{u}"], 16 * (i + (b - 3) // 2) + 16)
                        act.activation(attn[:, bass.ds(chunk(i, b, 3), 1), :].rearrange("p o d -> p (o d)"),
                                       PS[:, 6 + u, 256:384], ACT.Copy).then_inc(S["act_attn"], 1)
                    if has(0):
                        decays(1)
                        act.wait_ge(S["g_a"], n + 1)
                        wait(act, S["g_y"], n - 1)
                        act.activation(hid0[:, b, :], PS[:, 2, :], ACT.Tanh, scale=0.5 / WS).then_inc(S["g_tanh"], 1)
                    if has(2):
                        wait(act, S["act_ss"], n - 3)
                        act.wait_ge(S["dve_o"], n - 1)
                        act.activation(junk[:, b, :], o_sb[:, b, :], ACT.Square,
                                       accum_out=ssq[:, bass.ds(chunk(i, b, 2), 1)]).then_inc(S["act_ss"], 1)
                        act.wait_ge(S["pe_t"], n - 1)
                        wait(act, S["pe_w"], n - 3)
                        act.activation(oT[:, b, :], PS[:, 4 + b, 384:512], ACT.Copy).then_inc(S["act_ot"], 1)

            for u in range(2):
                act.wait_ge(S[f"qk_out{u}"], 16 * 6 * (NGRP // 2))
            act.wait_ge(S["qk_lo"], 2 * NGRP)
            act.wait_ge(S["k2_ready"], NGRP)
            loop(act, CPB, attend, peel=2)
            attend(CPB)
            act.wait_ge(S["pe_w"], NCH)
            act.wait_ge(S["scattered1"], 16 * CPB)
            act.activation(attn[:, NCH - 1, :], PS[:, 7, 256:384], ACT.Copy).then_inc(S["act_attn"], 1)
            act.wait_ge(S["act_ss"], NCH)
            act.activation(sdv, ssq, ACT.Sqrt, scale=1.0 / D, bias=eps_rms).then_inc(S["rms_sd"], 1)

            def sorted_hi(n, u):
                act.wait_ge(S["xs_ps"], n + 1)
                wait(act, S["f_b"], n - 1)
                wait(act, S["xs_lo"], n - 1)
                act.activation(xsh[:, u, :], PS[:, 6 + u, 0:P], ACT.Copy).then_inc(S["xs_hi"], 1)

            def silu_of(n, u):
                act.wait_ge(S["f_a"], n + 1)
                wait(act, S["f_h"], n - 1)
                act.activation(silu[:, u, :], PS[:, u, :], ACT.Silu, scale=1.0 / WS).then_inc(S["f_silu"], 1)

            def y_copy(n, u, turn):
                act.wait_ge(S["f_y"], n + 1)
                wait(act, S[f"y_out{u}"], 16 * turn)
                act.activation(ysb[:, u, :], PS[:, 4 + u, 0:D], ACT.Copy).then_inc(S["y_sb"], 1)

            def routed(i):
                for v in range(2):
                    n, u = 2 * i + 1 + v, (1 + v) % 2
                    sorted_hi(n + 1, 1 - u)
                    silu_of(n, u)
                    y_copy(n - 1, 1 - u, i)

            act.wait_ge(S["g_y"], NCH)
            sorted_hi(0, 0)
            sorted_hi(1, 1)
            silu_of(0, 0)
            loop(act, NBLK // 2 - 1, routed)
            silu_of(NBLK - 1, 1)
            y_copy(NBLK - 2, 0, NBLK // 2 - 1)
            y_copy(NBLK - 1, 1, NBLK // 2 - 1)

        @block.vector
        def _(dve):
            count = {}

            def link(ins, name):
                count[name] = count.get(name, 0) + 1
                ins.then_inc(S[name], 1)
                dve.wait_ge(S[name], count[name])

            dve.memset(eps_ln, LN_EPS).then_inc(S["eps_set"], 1)
            dve.memset(eps_rms, RMS_EPS * OS * OS).then_inc(S["eps_set"], 1)
            dve.memset(one, 1.0).then_inc(S["eps_set"], 1)
            dve.memset(lf[:, NCH * H:], 0.0)

            def norm(i):
                for u in range(2):
                    g = 2 * i + u
                    dve.wait_ge(S[f"x_in{u}"], 16 * i + 16)
                    for j in range(GRP):
                        last = dve.bn_stats(stats[:, u, j, :], x_sb[:, bass.ds(g * GRP + j, 1), :].rearrange("p o d -> p (o d)"))
                    last.then_inc(S["ln_stats"], 1)
                    dve.wait_ge(S["ln_stats"], g + 1)
                    for j in range(GRP):
                        last = dve.bn_aggr(mean_var[:, u, j, :], stats[:, u, j, :])
                    last.then_inc(S["ln_aggr"], 1)
                    gs = bass.ds(g * GRP, GRP)
                    dve.wait_ge(S["ln_sd"], g + 1)
                    dve.reciprocal(rstd[:, gs], sdv[:, gs]).then_inc(S["ln_rstd"], 1)
                    dve.wait_ge(S["ln_rstd"], g + 1)
                    for j in range(GRP):
                        c = bass.ds(g * GRP + j, 1)
                        last = dve.tensor_scalar(rows[:, c, 0:D].rearrange("p o d -> p (o d)"),
                                                 x_sb[:, c, :].rearrange("p o d -> p (o d)"),
                                                 mean_var[:, u, j, 0:1], rstd[:, c], ALU.subtract, ALU.mult)
                    last.then_inc(S["xn_ready"], 1)

            loop(dve, NGRP // 2, norm, peel=NGRP // 2)

            dve.wait_ge(S["logits_ready"], NGRP)
            dve.wait_ge(S["const_in"], 16 * NCONSTDMA)
            link(dve.tensor_tensor(zf, lg[:, :, E:E + H],
                                   delta_sb[:].unsqueeze(1).broadcast_to([P, NCH, H]), ALU.add), "forget")
            link(dve.tensor_scalar(zm, zf, 0.0, None, ALU.min), "forget")
            dve.scalar_tensor_tensor(ze, zm, 2.0, zf, ALU.mult, ALU.subtract).then_inc(S["forget_abs"], 1)
            link(dve.tensor_copy(rl, lg[:, :, 0:E]), "router")
            link(dve.tensor_reduce(rmax, rl, AX_X, ALU.max), "router")
            dve.tensor_tensor(rl, rl, rmax.unsqueeze(2).broadcast_to([P, NCH, E]), ALU.subtract).then_inc(S["router_in"], 1)
            dve.wait_ge(S["forget_ln"], 1)
            dve.tensor_tensor(lf[:, 0:NCH * H], zm.rearrange("p c h -> p (c h)"), ze.rearrange("p c h -> p (c h)"),
                              ALU.subtract).then_inc(S["lf_ready"], 1)
            dve.wait_ge(S["router_exp"], 1)
            dve.tensor_reduce(rsum, rexp, AX_X, ALU.add)
            link(dve.tensor_reduce(ptop, rexp[:, :, 1:E], AX_X, ALU.max), "router")
            dve.tensor_tensor(eq, rexp[:, :, 1:E], ptop.unsqueeze(2).broadcast_to([P, NCH, R]), ALU.is_equal)
            link(dve.tensor_tensor(den, rexp[:, :, 0], ptop, ALU.add), "router")
            link(dve.scalar_tensor_tensor(den2, rsum, 1e-9, den, ALU.mult, ALU.max), "router")
            link(dve.reciprocal(den, den2), "router")
            dve.scalar_tensor_tensor(g0, rexp[:, :, 0], 0.5 / (WS * WS), den, ALU.mult, ALU.mult).then_inc(S["gates"], 1)
            dve.scalar_tensor_tensor(g1, ptop, 1.0 / WS, den, ALU.mult, ALU.mult).then_inc(S["gates"], 1)
            link(dve.tensor_tensor(eq, eq, cc("order").unsqueeze(1).broadcast_to([P, NCH, R]), ALU.mult), "router")
            link(dve.tensor_reduce(oscore, eq, AX_X, ALU.max), "router")
            dve.tensor_tensor(oh, eq, oscore.unsqueeze(2).broadcast_to([P, NCH, R]), ALU.is_equal).then_inc(S["onehot"], 1)
            dve.wait_ge(S["rank_ps"], 1)
            link(dve.tensor_copy(tt, ntok_ps), "router")
            link(dve.tensor_tensor_scan(incl.rearrange("p e c -> p (e c)"), cc("scan0"),
                                        tt.rearrange("p e c -> p (e c)"), 0.0, ALU.mult, ALU.add), "router")
            link(dve.tensor_tensor(off, incl[:, :, NCH - 1:NCH].broadcast_to([P, R, NCH]),
                                   cc("fill").unsqueeze(1).broadcast_to([P, R, NCH]), ALU.is_gt), "router")
            link(dve.tensor_reduce(nblk[:, 0, :], off, AX_X, ALU.add), "router")
            link(dve.tensor_tensor_scan(nblk[:, 1, :], cc("one7"), nblk[:, 0, :], 0.0, ALU.mult, ALU.add), "router")
            link(dve.tensor_tensor(nblk[:, 2, :], nblk[:, 1, :], nblk[:, 0, :], ALU.subtract), "router")
            link(dve.tensor_tensor(off, incl, tt, ALU.subtract), "router")
            link(dve.scalar_tensor_tensor(off, nblk[:, 2, :].unsqueeze(2).broadcast_to([P, R, NCH]), float(P), off,
                                          ALU.mult, ALU.add), "router")
            link(dve.tensor_tensor(eq, rank_ps, off.rearrange("p e c -> p c e"), ALU.add), "router")
            link(dve.tensor_tensor(eq, eq, oh, ALU.mult), "router")
            link(dve.tensor_reduce(slot, eq, AX_X, ALU.add), "router")
            dve.tensor_copy(slot_i[:], slot).then_inc(S["slots"], 1)
            link(dve.tensor_tensor(bcmp, cc("blk")[0:1].unsqueeze(2).broadcast_to([1, NBLK, R - 1]),
                                   nblk[0:1, 1, 0:R - 1].unsqueeze(1).broadcast_to([1, NBLK, R - 1]), ALU.is_ge), "router")
            link(dve.tensor_reduce(bsum, bcmp, AX_X, ALU.add), "router")
            dve.tensor_scalar(expert[:], bsum, 1.0, None, ALU.add).then_inc(S["blocks_known"], 1)

            dve.wait_ge(S["lbT_sb"], 1)
            dve.wait_ge(S["tot_ps"], 1)
            for p in range(3):
                dve.tensor_copy(lbS[:, p, :], lbT).then_inc(S["lb_parts"], 1)
                if p < 2:
                    dve.wait_ge(S["lb_parts"], p + 1)
                    link(dve.tensor_tensor(lbT, lbT, lbS[:, p, :], ALU.subtract), "lb_rest")

            dve.wait_ge(S["wq_hi"], 1)
            dve.scalar_tensor_tensor(wql[:], wraw.rearrange("p w d -> p (w d)"), WS, wqh[:],
                                     ALU.mult, ALU.subtract).then_inc(S["wq_lo"], 1)
            dve.tensor_scalar(wo_sb[:], wo_raw, nw_sb[:, 0:1], None, ALU.mult).then_inc(S["wo_ready"], 1)

            def low_w(i):
                for u in range(2):
                    e = bass.ds(2 * i + u, 1)
                    dve.wait_ge(S["w_hi"], 2 * i + u + 1)
                    dve.scalar_tensor_tensor(w13h[:, e, :, 1, :].rearrange("p o w f -> p (o w) f"), wstage[:, u, :, :], WS,
                                             w13h[:, e, :, 0, :].rearrange("p o w f -> p (o w) f"),
                                             ALU.mult, ALU.subtract).then_inc(S["w_lo"], 1)

            loop(dve, E // 2, low_w)

            dve.wait_ge(S["lb_moved"], 16 * 36)
            dve.wait_ge(S["w_lo"], E)
            dve.wait_ge(S["slots"], 1)
            dve.wait_ge(S["blocks_known"], 1)
            dve.wait_ge(S["xl_ready"], NGRP)
            dve.wait_ge(S["init_out"], 16)

            def gate(i):
                for u in range(2):
                    g = 2 * i + u
                    cols = bass.ds(g * GRP * P, GRP * P)
                    dve.wait_ge(S["qk_tanh"], g + 1)
                    dve.scalar_tensor_tensor(qT[:, cols], tq[:, u, 0, :], 1.0, PS[:, 4 * u, :], ALU.add, ALU.mult
                                             ).then_inc(S["qk_f32"], 1)
                    wait(dve, S["qk_hi"], 2 * g - 2)
                    wait(dve, S["qk_lo"], 2 * g - 2)
                    dve.scalar_tensor_tensor(kT[:, u, :], tq[:, u, 1, :], 1.0, PS[:, 4 * u + 1, :], ALU.add, ALU.mult
                                             ).then_inc(S["qk_f32"], 1)
                    dve.wait_ge(S["k_tanh"], g + 1)
                    dve.wait_ge(S["v_ready"], g + 1)
                    kv = PS[:, 4 * u + 2:4 * u + 4, :].rearrange("p b (c n) -> p b c n", n=2 * D)
                    dve.scalar_tensor_tensor(k2[:, bass.ds(g * GRP, GRP), :].rearrange("p (b c) d -> p b c d", c=2),
                                             tk[:, u].rearrange("p (b c) d -> p b c d", c=2), 1.0, kv[:, :, :, 0:D],
                                             ALU.add, ALU.mult).then_inc(S["k2_ready"], 1)
                    dve.wait_ge(S["qk_f32"], 2 * g + 2)
                    wait(dve, S[f"qk_out{u}"], 16 * 6 * i)
                    for t, src in ((0, qT[:, cols]), (1, kT[:, u, :])):
                        dve.wait_ge(S["qk_hi"], 2 * g + 1 + t)
                        dve.tensor_tensor(qkl[:, u, t, :], src, qkh[:, u, t, :], ALU.subtract).then_inc(S["qk_lo"], 1)

            loop(dve, NGRP // 2, gate)

            for u in range(2):
                dve.wait_ge(S[f"qk_out{u}"], 16 * 6 * (NGRP // 2))
            dve.wait_ge(S["decays"], 3)
            dve.wait_ge(S["gates"], 2)
            dve.wait_ge(S["qk_lo"], 2 * NGRP)
            link(dve.memset(state[:, :, 0, :], 0.0), "state_zero")

            def finish(i, b):
                n = 2 * i + b
                u, c = (b - 1) % 2, chunk(i, b, 1)
                dve.wait_ge(S["pe_i"], n)
                dve.wait_ge(S["dve_s1"], n)
                dve.scalar_tensor_tensor(state[:, u, 0, :], state[:, u, 1, :], dec[:, bass.ds(c * NS + 1, 1)],
                                         um[:, u, 1, :], ALU.mult, ALU.add).then_inc(S["dve_s0"], 1)
                dve.wait_ge(S["pe_av"], n)
                wait(dve, S["dve_o"], n - 1)
                dve.tensor_tensor(o1.rearrange("p (h d) -> p h d", d=HD),
                                  PS[:, 4 + u, 256:384].rearrange("p (h d) -> p h d", d=HD),
                                  elb[:, bass.ds(c, 1), :].rearrange("p o h -> p (o h)").unsqueeze(2).broadcast_to([P, H, HD]),
                                  ALU.mult).then_inc(S["dve_o1"], 1)
                dve.wait_ge(S["dve_o1"], n)
                wait(dve, S["pe_t"], n - 2)
                wait(dve, S["act_ss"], n - 2)
                av = PS[0:SUB, 4 + u, 0:2 * D].rearrange("p (h s e) -> p h s e", s=NS, e=HD)
                for s in range(NS):
                    tok = slice(s * SUB, (s + 1) * SUB)
                    last = dve.tensor_tensor(o_sb[tok, u, :].rearrange("p (h e) -> p h e", e=HD),
                                             o1[tok, :].rearrange("p (h e) -> p h e", e=HD),
                                             av[:, :, s, :], ALU.add)
                last.then_inc(S["dve_o"], 1)
                dve.wait_ge(S["g_y"], n)
                cx = bass.ds(n - 1, 1)
                x_rows = x_sb[:, cx, :].rearrange("p o d -> p (o d)")
                dve.scalar_tensor_tensor(x_rows, PS[:, 6 + u, 384:512], g0[:, cx], x_rows,
                                         ALU.mult, ALU.add).then_inc(S["dve_y"], 1)

            def attend(i):
                for b in range(2):
                    n, c = 2 * i + b, chunk(i, b)
                    for half in range(2):
                        dve.wait_ge(S["act_e"], 2 * n + half + 1)
                        dve.wait_ge(S["pe_a"], 2 * n + half + 1)
                        wait(dve, S["pe_av"], n - 1)
                        dve.tensor_tensor(pbuf[:, b, half * 512:(half + 1) * 512], ebuf[:, half, :], PS[:, 1, :],
                                          ALU.mult).then_inc(S["dve_p"], 1)
                    dve.wait_ge(S["g_tanh"], n + 1)
                    dve.scalar_tensor_tensor(hid0[:, b, :], hid0[:, b, :], 1.0, PS[:, 2, :], ALU.add, ALU.mult
                                             ).then_inc(S["g_silu"], 1)
                    dve.wait_ge(S["g_silu"], n + 1)
                    dve.wait_ge(S["g_b"], n + 1)
                    dve.tensor_tensor(hid0[:, b, :], hid0[:, b, :], PS[:, 3, :], ALU.mult).then_inc(S["g_h"], 1)
                    dve.wait_ge(S["pe_u"], n + 1)
                    wait(dve, S["dve_s0"], n - 1)
                    dve.tensor_tensor(um[:, b].rearrange("p s (h e) -> p s h e", e=HD),
                                      PS[:, 6 + b, 0:2 * D].rearrange("p (h s e) -> p s h e", s=NS, e=HD),
                                      cc("hmask").unsqueeze(1).unsqueeze(3).broadcast_to([P, NS, H, HD]),
                                      ALU.mult).then_inc(S["dve_um"], 1)
                    dve.wait_ge(S["dve_um"], n + 1)
                    wait(dve, S["pe_i"], n - 1)
                    dve.scalar_tensor_tensor(state[:, b, 1, :], state[:, b, 0, :], dec[:, bass.ds(c * NS, 1)],
                                             um[:, b, 0, :], ALU.mult, ALU.add).then_inc(S["dve_s1"], 1)
                    if not (isinstance(n, int) and n == 0):
                        finish(i, b)

            loop(dve, CPB, attend, peel=2)
            finish(CPB, 0)

            dve.wait_ge(S["rms_sd"], 1)
            link(dve.reciprocal(rstd, sdv), "rms")

            def sorted_lo(n, u, turn):
                dve.wait_ge(S[f"xrow_in{u}"], 16 * turn + 16)
                dve.tensor_copy(ids[:, bass.ds(n, 1)], xrow[:, u, D:ROW].bitcast(I32)).then_inc(S["id_copied"], 1)
                dve.wait_ge(S["xs_hi"], n + 1)
                wait(dve, S["f_b"], n - 1)
                dve.tensor_tensor(xsl[:, u, :], PS[:, 6 + u, 0:P], xsh[:, u, :], ALU.subtract).then_inc(S["xs_lo"], 1)

            def hidden(n, u):
                dve.wait_ge(S["f_silu"], n + 1)
                dve.wait_ge(S["f_b"], n + 1)
                wait(dve, S["f_y"], n - 1)
                dve.tensor_tensor(hid[:, u, :], silu[:, u, :], PS[:, 2 + u, :], ALU.mult).then_inc(S["f_h"], 1)

            def routed(i):
                for v in range(2):
                    n, u = 2 * i + 1 + v, (1 + v) % 2
                    sorted_lo(n + 1, 1 - u, i + 1)
                    hidden(n, u)

            dve.wait_ge(S["pe_w"], NCH)
            sorted_lo(0, 0, 0)
            sorted_lo(1, 1, 0)
            hidden(0, 0)
            loop(dve, NBLK // 2 - 1, routed)
            hidden(NBLK - 1, 1)

            dve.wait_ge(S["x_done"], NCH)
            for q in range(NQ):
                dve.wait_ge(S[f"yt_in{q}"], 16)
                for c in range(NCH)[quarter(q)]:
                    dve.scalar_tensor_tensor(yt[:, c, :], yt[:, c, :], g1[:, c:c + 1], x_sb[:, c, :],
                                             ALU.mult, ALU.add).then_inc(S["dve_out"], 1)

        @block.tensor
        def _(pe):
            def mm(out_, lhsT, rhs, start=True, stop=True):
                return pe.matmul(out_, lhsT, rhs, start=start, stop=stop)

            def split_product(out_, a_hi, a_lo, b_hi, b_lo):
                mm(out_, a_hi, b_hi, True, False)
                mm(out_, a_hi, b_lo, False, False)
                return mm(out_, a_lo, b_hi, False, True)

            pe.wait_ge(S["const_in"], 16 * NCONSTDMA)

            for g in range(NGRP):
                u = g % 2
                pe.wait_ge(S["xn_ready"], g + 1)
                wait(pe, S["xh_ready"], g - 1)
                for j in range(GRP):
                    last = pe.transpose(PS[:, u, j * P:(j + 1) * P], rows[:, g * GRP + j, 0:D], cc("ident"))
                last.then_inc(S["xnT_ps"], 1)
                pe.wait_ge(S["xnT_sb"], g + 1)
                for j in range(GRP):
                    last = mm(lg[:, g * GRP + j, 0:E + H], xnT[:, u, j * P:(j + 1) * P], wrf_sb[:])
                last.then_inc(S["logits_ready"], 1)

            pe.wait_ge(S["lf_ready"], 1)
            flat = lf[:, 0:NCH * H]
            mm(PS[:, 5, :], cc("cum"), flat)
            mm(PS[:, 6, :], cc("suffix"), flat).then_inc(S["cum_ps"], 1)
            pe.wait_ge(S["xh_ready"], NGRP)
            for c in range(NCH):
                k, col = c // 8, (c % 8) * P
                last = mm(PS[32 * k:32 * k + 32, col // 512, col % 512:col % 512 + P],
                          lf[:, c * H:c * H + 32], cc("cum"))
            last.then_inc(S["lbT_ps"], 1)
            pe.wait_ge(S["lbT_sb"], 1)
            pe.wait_ge(S["router_in"], 1)
            for k in range(4):
                rows_k = slice(32 * k, 32 * k + H)
                last = mm(PS[:, k, 0:NCH * NS // 4], cc("expand")[rows_k],
                          lbT[rows_k, :].rearrange("p (n i) -> p n i", i=SUB)[:, :, SUB - 1])
            last.then_inc(S["tot_ps"], 1)
            pe.wait_ge(S["onehot"], 1)
            flat = oh.rearrange("p c e -> p (c e)")
            mm(PS[:, 4, 0:NCH * R], cc("rank"), flat)
            mm(PS[:, 4, NCH * R:2 * NCH * R], cc("ones"), flat).then_inc(S["rank_ps"], 1)

            pe.wait_ge(S["decays"], 3)
            pe.wait_ge(S["slots"], 1)
            pe.wait_ge(S["wq_lo"], 1)
            pe.wait_ge(S["xl_ready"], NGRP)

            def project(i):
                for u in range(2):
                    g = 2 * i + u
                    cols = bass.ds(g * GRP * P, GRP * P)
                    wait(pe, S["qk_f32"], 2 * g - 2)
                    for t in range(2):
                        w = slice(t * D, (t + 1) * D)
                        last = split_product(PS[:, 4 * u + t, :], wqh[:, w], wql[:, w], xh[:, cols], xl[:, cols])
                    last.then_inc(S["q_ps"], 1)
                    wait(pe, S["k2_ready"], g - 1)
                    wait(pe, S["v_ready"], g - 1)
                    for j in range(GRP):
                        tok = bass.ds(g * GRP * P + j * P, P)
                        last = split_product(PS[:, 4 * u + 2 + j // 2, (j % 2) * 2 * D:(j % 2 + 1) * 2 * D],
                                             xh[:, tok], xl[:, tok], wqh[:, D:3 * D], wql[:, D:3 * D])
                    last.then_inc(S["kv_ps"], 1)

            loop(pe, NGRP // 2, project)

            def up(e, w, bank, hi, lo):
                for f in range(FB):
                    cols = slice(f * P, (f + 1) * P)
                    wt = [w13h[:, bass.ds(e, 1), w, part, cols].rearrange("p o f -> p (o f)") for part in range(2)]
                    last = split_product(PS[:, bank, cols], wt[0], wt[1], hi, lo)
                return last

            def down(weights, hidden, out_):
                for f in range(FB):
                    last = mm(out_, hidden[:, f * P:(f + 1) * P], weights[:, f, :], f == 0, f == FB - 1)
                return last

            pe.wait_ge(S["w_lo"], E)
            pe.wait_ge(S["qk_f32"], 2 * NGRP)
            pe.wait_ge(S["k2_ready"], NGRP)
            pe.wait_ge(S["v_ready"], NGRP)
            pe.wait_ge(S["dstat_in"], 16 * 5)
            pe.wait_ge(S["wo_ready"], 1)
            pe.wait_ge(S["state_zero"], 1)

            def attend(i):
                for b in range(2):
                    n = 2 * i + b
                    known = isinstance(n, int)

                    def has(k):
                        return not known or 0 <= n - k < NCH

                    u = 1 - b
                    if has(0):
                        def weights(half):
                            pe.wait_ge(S[f"dr_in{b}"], 16 * i + 16)
                            wait(pe, S["act_e"], 2 * n + half)
                            mm(PS[:, 0, :], dL[:, bass.ds(chunk(i, b), 1), :].rearrange("p o t -> p (o t)"),
                               dR[:, b, half * 512:(half + 1) * 512]).then_inc(S["pe_d"], 1)
                            pe.wait_ge(S[f"st_in{b}"], 32 * i + 32)
                            wait(pe, S["dve_p"], 2 * n + half)
                            for h in range(half * H // 2, (half + 1) * H // 2):
                                for s in range(NS):
                                    tok = slice(s * SUB, (s + 1) * SUB)
                                    last = mm(PS[tok, 1, (h % 8) * SUB:(h % 8 + 1) * SUB],
                                              k_st[:, b, h, tok], q_st[:, b, h, tok])
                            last.then_inc(S["pe_a"], 1)

                        weights(0)
                        tok = bass.ds(n * P, P)
                        wait(pe, S["g_silu"], n)
                        up(0, 0, 2, xh[:, tok], xl[:, tok]).then_inc(S["g_a"], 1)
                        wait(pe, S["g_h"], n)
                        up(0, 1, 3, xh[:, tok], xl[:, tok]).then_inc(S["g_b"], 1)
                        weights(1)
                    if has(2):
                        pe.wait_ge(S["dve_o"], n - 1)
                        wait(pe, S["act_ot"], n - 3)
                        pe.transpose(PS[:, 4 + b, 384:512], o_sb[:, b, :], cc("ident")).then_inc(S["pe_t"], 1)
                    if has(0):
                        pe.wait_ge(S["pool_kd"], n + 1)
                        pe.wait_ge(S["pool_v2"], n + 1)
                        wait(pe, S["dve_um"], n - 1)
                        wait(pe, S["act_attn"], n - 3)
                        wait(pe, S["dve_y"], n - 1)
                        mm(PS[:, 6 + b, 0:2 * D], kd[:, b, :], v2[:, b, :]).then_inc(S["pe_u"], 1)
                    if has(1):
                        pe.wait_ge(S["dve_s1"], n)
                        wait(pe, S["dve_s0"], n - 2)
                        wait(pe, S["dve_o"], n - 2)
                        wait(pe, S["act_ot"], n - 2)
                        pe.wait_ge(S[f"q_in{u}"], 16 * (i + (b - 1) // 2) + 16)
                        for s in range(NS):
                            tok = slice(s * SUB, (s + 1) * SUB)
                            last = mm(PS[tok, 4 + u, 256:384], q_now[:, u, tok], state[:, u, s, :])
                        last.then_inc(S["pe_i"], 1)
                        pe.wait_ge(S["dve_p"], 2 * n)
                        for h in range(H):
                            last = mm(PS[0:SUB, 4 + u, h * NS * HD:(h + 1) * NS * HD],
                                      pbuf[:, u, h * SUB:(h + 1) * SUB], v2[:, u, h * NS * HD:(h + 1) * NS * HD])
                        last.then_inc(S["pe_av"], 1)
                        pe.wait_ge(S["g_h"], n)
                        wait(pe, S["act_attn"], n - 2)
                        down(w2_first[:], hid0[:, u, :], PS[:, 6 + u, 384:512]).then_inc(S["g_y"], 1)
                    if has(2):
                        pe.wait_ge(S["act_ot"], n - 1)
                        pe.wait_ge(S["dve_um"], min(n + 1, NCH) if known else n + 1)
                        pe.wait_ge(S["dve_y"], n - 1)
                        mm(PS[:, 6 + b, 256:384], oT[:, b, :], wo_sb[:]).then_inc(S["pe_w"], 1)

            loop(pe, CPB, attend, peel=2)
            attend(CPB)

            def turn_rows(n, u, turn):
                pe.wait_ge(S[f"xrow_in{u}"], 16 * turn + 16)
                wait(pe, S["xs_lo"], n - 1)
                pe.transpose(PS[:, 6 + u, 0:P], xrow[:, u, 0:D], cc("ident")).then_inc(S["xs_ps"], 1)

            block_expert = [pe.alloc_register(f"block_expert{k}") for k in range(3)]

            def experts_of(n, count):
                pe.load(block_expert[:count], expert[0:1, bass.ds(n, count)])
                return [pe.snap(reg, min_val=1, max_val=E - 1) for reg in block_expert[:count]]

            def up_routed(n, u, e):
                pe.wait_ge(S["xs_hi"], n + 1)
                pe.wait_ge(S["xs_lo"], n + 1)
                wait(pe, S["f_silu"], n - 1)
                wait(pe, S["f_h"], n - 1)
                for w in range(2):
                    up(e, w, 2 * w + u, xsh[:, u, :], xsl[:, u, :]).then_inc(S["f_" + "ab"[w]], 1)

            def down_routed(n, u, e):
                pe.wait_ge(S["f_h"], n + 1)
                wait(pe, S["y_sb"], n - 1)
                down(w2_sb[:, bass.ds(e, 1)].rearrange("p o f d -> p (o f) d"), hid[:, u, :], PS[:, 4 + u, 0:D]
                     ).then_inc(S["f_y"], 1)

            pe.wait_ge(S["act_attn"], NCH)
            pe.wait_ge(S["dve_y"], NCH)
            pe.wait_ge(S["w2_in"], 16)
            turn_rows(0, 0, 0)
            turn_rows(1, 1, 0)
            up_routed(0, 0, experts_of(0, 1)[0])

            def routed(i):
                e = experts_of(2 * i, 3)
                for v in range(2):
                    n, u = 2 * i + 1 + v, (1 + v) % 2
                    turn_rows(n + 1, 1 - u, i + 1)
                    up_routed(n, u, e[v + 1])
                    down_routed(n - 1, 1 - u, e[v])

            loop(pe, NBLK // 2 - 1, routed)
            e = experts_of(NBLK - 2, 2)
            up_routed(NBLK - 1, 1, e[1])
            down_routed(NBLK - 2, 0, e[0])
            down_routed(NBLK - 1, 1, e[1])


def kernel(L0_attn_x, L0_attn_Wq, L0_attn_Wk, L0_attn_Wv, L0_attn_Wo, L0_attn_Wf, L0_attn_delta,
           L0_attn_norm_weight, L0_ffn_Wr, L0_ffn_W1, L0_ffn_W2, L0_ffn_W3):
    import concourse.bacc as bacc
    from concourse.bass_utils import run_bass_kernel_spmd

    dleft, dright = decay_constants()
    arrays = {
        "x": np.ascontiguousarray(L0_attn_x).reshape(TOK, D),
        "wqkv": np.ascontiguousarray(np.stack([np.asarray(w).T for w in (L0_attn_Wq, L0_attn_Wk, L0_attn_Wv)], 1)),
        "wo": np.ascontiguousarray(np.asarray(L0_attn_Wo).T),
        "wrf": np.ascontiguousarray(np.concatenate([np.asarray(L0_ffn_Wr), np.asarray(L0_attn_Wf)], 0).T),
        "delta": np.ascontiguousarray(L0_attn_delta),
        "nw": np.ascontiguousarray(L0_attn_norm_weight).reshape(D, 1),
        "w13": np.ascontiguousarray(np.stack([np.asarray(L0_ffn_W1), np.asarray(L0_ffn_W3)], 1).transpose(3, 0, 1, 2)),
        "w2": np.ascontiguousarray(np.asarray(L0_ffn_W2).reshape(E, D, FB, P).transpose(3, 0, 2, 1)),
        "const": constants(),
        "dleft": dleft,
        "dright": dright,
    }
    nc = bacc.Bacc("TRN2", target_bir_lowering=False, num_devices=1)
    args = [nc.dram_tensor(n, a.shape, mybir.dt.from_np(a.dtype), kind="ExternalInput").ap() for n, a in arrays.items()]
    args.append(nc.dram_tensor("out", (TOK, D), F32, kind="ExternalOutput").ap())
    for n, shape, dt in (("qk_scr", (2, 3, HD, H, TOK), F16), ("lb_scr", (NCH, 3, NS, H, SUB), BF16),
                         ("xsort", (NBLK * P, ROW), F32), ("ytok", (TOK + NBLK * P, D), F32)):
        args.append(nc.dram_tensor(n, shape, dt, kind="Internal").ap())
    build(nc, *args)
    r = run_bass_kernel_spmd(nc, [arrays], core_ids=[0])
    return np.asarray(r.results[0]["out"]).reshape(BATCH, SEQ, D)
```

```python
from contextlib import ExitStack

import numpy as np
import concourse.bass as bass
from concourse import mybir

F32 = mybir.dt.float32
F16 = mybir.dt.float16
BF16 = mybir.dt.bfloat16
I32 = mybir.dt.int32
ALU = mybir.AluOpType
ACT = mybir.ActivationFunctionType
AX_X = mybir.AxisListType.X

P = 128
BATCH, SEQ, D = 2, 2048, 128
TOK = BATCH * SEQ
NCH = TOK // P
CPB = NCH // BATCH
H, HD = 16, 8
SUB = 64
NS = P // SUB
E, FF = 8, 512
FB = FF // P
R = E - 1
GRP = 4
NGRP = NCH // GRP
NBLK = NCH + R - 1
ROW = D + 1
LN_EPS, RMS_EPS = 1e-5, 1e-6
WS = 64.0
QS = 2.0 * WS
OS = QS * QS * WS
BIG = -1.0e30
DROWS = 3 * H + 3 * NS + SUB
NLB, NSEL = 3 * H, 3 * NS

COLS = {}
_at = 0
for _name, _n in [("ident", P), ("hmask", H), ("smask", NS),
                  ("rank", P), ("ones", P), ("cum", P), ("suffix", P), ("expand", P),
                  ("scan0", R * NCH), ("one7", R), ("order", R), ("fill", NCH), ("blk", NBLK)]:
    COLS[_name] = (_at, _at + _n)
    _at += _n
NCONST = _at
NKEPT = COLS["smask"][1]


def constants():
    k = np.arange(P)[:, None]
    m = np.arange(P)[None, :]
    same = (k // SUB) == (m // SUB)
    c = np.zeros((P, NCONST), np.float32)

    def put(name, v):
        a, b = COLS[name]
        c[:, a:b] = v

    put("rank", k < m)
    put("ones", 1)
    put("cum", (k <= m) & same)
    put("suffix", (k > m) & same)
    put("ident", k == m)
    put("expand", (k % 32 == m % H))
    put("scan0", (np.arange(R * NCH) % NCH != 0)[None])
    put("one7", 1)
    put("order", (R - np.arange(R))[None])
    put("fill", (P * np.arange(NCH))[None])
    put("blk", np.arange(NBLK)[None])
    put("hmask", k % H == np.arange(H)[None])
    put("smask", k // SUB == np.arange(NS)[None])
    return c


def decay_constants():
    j = np.arange(P)
    left = np.zeros((NSEL + SUB, P), np.float32)
    for p in range(3):
        for s in range(NS):
            left[p * NS + s] = (j // SUB == s)
    left[NSEL:] = (np.arange(SUB)[:, None] == (j % SUB)[None])
    right = np.zeros((DROWS, H, SUB), np.float32)
    for p in range(3):
        for h in range(H):
            right[p * H + h, h] = -1
    right[NLB + NSEL:] = np.where(np.arange(SUB)[None, None, :] < np.arange(SUB)[:, None, None], BIG, 0)

    def bits(a):
        return (np.ascontiguousarray(a).view(np.uint32) >> 16).astype(np.uint16)

    return bits(left), bits(right.reshape(DROWS, H * SUB))


def build(nc, x, wqkv, wo, wrf, delta, nw, w13, w2, const, dleft, dright, out,
          qk_scr, lb_scr, xsort, ytok):
    dleft, dright = dleft.bitcast(BF16), dright.bitcast(BF16)
    with ExitStack() as ctx:
        def sb(name, shape, dt=F32):
            return ctx.enter_context(nc.sbuf_tensor(name, shape, dt))

        def sem(name):
            return ctx.enter_context(nc.semaphore(name))

        def wait(eng, s, value):
            if isinstance(value, int) and value <= 0:
                return
            eng.wait_ge(s, value)

        def at(eng, value):
            return value if isinstance(value, int) else eng.snap(value)

        def loop(eng, count, body, peel=1, start=0):
            for i in range(start, start + peel):
                body(i)
            if start + peel < count:
                with eng.Fori(start + peel, count) as i:
                    body(i)

        class Region:

            def __init__(self, name, kib):
                self.tensor, self.at, self.size = sb(name, [P, kib * 256]), 0, kib * 256

            def take(self, shape, dt=F32):
                per = 1 if dt in (F32, I32) else 2
                n = int(np.prod(shape[1:]))
                words = -(-n // per)
                a = self.at
                self.at += words
                assert self.at <= self.size, (self.at, self.size)
                v = self.tensor[0:shape[0], a:a + words]
                if dt != F32:
                    v = v.bitcast(dt)
                names = "abcd"[:len(shape) - 1]
                if len(shape) > 2:
                    v = v.rearrange(f"p ({' '.join(names)}) -> p {' '.join(names)}",
                                    **{k: m for k, m in zip(names[1:], shape[2:])})
                return v

            def again(self, at=0):
                self.at = at

        PS = ctx.enter_context(nc.psum_tensor("PS", [P, 8, 512], F32))
        kept_cst = sb("kept_cst", [P, NKEPT])
        w2_first = sb("w2_first", [P, FB, D])
        x_sb = sb("x_sb", [P, NCH, D])
        rows = sb("rows", [P, NCH, ROW])
        attn = rows[:, :, 0:D]
        xh = sb("xh", [P, TOK], F16)
        xl = sb("xl", [P, TOK], F16)
        w13h = sb("w13h", [P, E, 2, 2, FF], F16)
        elb = sb("elb", [P, NCH, H])
        sdec = sb("sdec", [P, NCH, H])
        dec = sb("dec", [P, NCH * NS])
        small = sb("small", [P, 12, NCH])
        mean_var = sb("mean_var", [P, 2, GRP, 2])
        stats = sb("stats", [P, 2, GRP, 6])
        g0, g1, ssq, sdv, rstd = (small[:, k, :] for k in range(5))
        rmax, rsum, ptop, den, den2, oscore, slot = (small[:, k, :] for k in range(5, 12))
        slot_i = sb("slot_i", [P, NCH], I32)
        expert = sb("expert", [1, NBLK], I32)
        ids = sb("ids", [P, NBLK], I32)
        eps = sb("eps", [P, 3])
        eps_ln, eps_rms, one = eps[:, 0:1], eps[:, 1:2], eps[:, 2:3]
        wrf_sb = sb("wrf_sb", [P, E + H])
        delta_sb = sb("delta_sb", [P, H])
        nw_sb = sb("nw_sb", [P, 1])
        wo_sb = sb("wo_sb", [P, D])
        wqh = sb("wqh", [P, 3 * D], F16)
        wql = sb("wql", [P, 3 * D], F16)

        Z = Region("Z", 48)
        early_cst = Z.take([P, NCONST - NKEPT])
        lf = Z.take([P, (NCH + 1) * H])
        wraw = Z.take([P, 3, D])
        wo_raw = Z.take([P, D])
        rl = Z.take([P, NCH, E])
        rexp = Z.take([P, NCH, E])
        eq = Z.take([P, NCH, R])
        oh = Z.take([P, NCH, R])
        tt = Z.take([P, R, NCH])
        incl = Z.take([P, R, NCH])
        off = Z.take([P, R, NCH])
        bcmp = Z.take([1, NBLK, R - 1])
        bsum = Z.take([1, NBLK])
        nblk = Z.take([P, 3, R])
        zf = Z.take([P, NCH, H])
        zm = Z.take([P, NCH, H])
        ze = Z.take([P, NCH, H])
        wstage = Z.take([P, 4, 2, FF])
        Z.again()
        qT = Z.take([P, TOK])
        k2 = Z.take([P, NCH, D])
        v_sb = Z.take([P, NCH, D])
        Z.again()
        w2_sb = Z.take([P, E, FB, D])

        def cc(name):
            a, b = COLS[name]
            return kept_cst[:, a:b] if b <= NKEPT else early_cst[:, a - NKEPT:b - NKEPT]

        C = Region("C", 44)
        xnT = C.take([P, 2, GRP * P])
        zero = C.take([P, NBLK, ROW])
        C.again()
        kT = C.take([P, 4, GRP * P])
        parts = C.take([P, 4, GRP, 4, P], F16)
        parts_end = C.at
        lbT = C.take([P, 8 * P])
        lbS = C.take([P, 3, 8 * P], BF16)
        lb_end = C.at
        C.again()
        ebuf = C.take([P, 2, H * SUB // 2])
        state = C.take([P, 2, NS, D])
        kd = C.take([P, 2, D])
        o1 = C.take([P, 2 * D])[:, 0:D]
        pbuf = C.take([P, 2, H * SUB])
        qk_odd = C.take([3 * HD, 2, H * P], F16)
        assert C.at == parts_end
        hid0 = C.take([P, 2, FF])
        v2 = C.take([P, 2, H * NS * HD])
        um = C.take([P, 2, NS, D])
        q_now = C.take([P, 2, P])
        o_sb = C.take([P, 2, D])
        squares = C.take([P, 2, D])
        oT = C.take([P, 2, D])
        late = C.at
        assert late >= lb_end
        qk_even = C.take([3 * HD, 2, H * P], F16)
        qk_st = (qk_even, qk_odd)
        C.again()
        silu = C.take([P, 2, FF])
        hid = C.take([P, 2, FF])
        ysb = C.take([P, 2, D])
        yt = C.take([P, NCH, D])
        C.again(late)
        xrow = C.take([P, 2, ROW])
        xsh = C.take([P, 2, P], F16)
        xsl = C.take([P, 2, P], F16)
        dL = sb("dL", [DROWS, NCH, P], BF16)
        dR = sb("dR", [DROWS, 2, H * SUB], BF16)

        class Sems(dict):
            def __missing__(self, name):
                self[name] = sem(name)
                return self[name]

        S = Sems()
        NCONSTDMA = 4

        lg = PS[:, 2:4, :].rearrange("p b (c n) -> p (b c) n", n=2 * 512 // NCH)
        rank_ps = PS[:, 4, 0:NCH * R].rearrange("p (c e) -> p c e", e=R)
        ntok_ps = PS[:, 4, NCH * R:2 * NCH * R].rearrange("p (c e) -> p e c", e=R)

        def chunk(i, b, k=0):
            return ((b - k) % 2) * CPB + i + (b - k) // 2

        LEAD = 4
        NQ = 8

        def share(q):
            return slice(q * NCH // NQ, (q + 1) * NCH // NQ)

        block = ctx.enter_context(nc.Block())

        @block.sync
        def _(sp):
            def load_x(i):
                for u in range(4):
                    gs = bass.ds(at(sp, (4 * i + u) * GRP), GRP)
                    wait(sp, S[f"x_in{u}"], 16 * i)
                    sp.dma_start(x_sb[:, gs, :], x.rearrange("(c p) d -> p c d", p=P)[:, gs, :]
                                 ).then_inc(S[f"x_in{u}"], 16)

            loop(sp, NGRP // 4, load_x)

            def load_w(i):
                for u in range(4):
                    e = at(sp, 4 * i + u)
                    wait(sp, S["w_lo"], 4 * i + u - 3)
                    sp.dma_start(wstage[:, u, :, :], w13[:, bass.ds(e, 1)].rearrange("p o w f -> p (o w) f")
                                 ).then_inc(S[f"stage_in{u}"], 16)

            load_w(0)
            for dst, src in ((w2_first[:], w2[:, 0]), (nw_sb[:], nw), (wo_raw, wo), (wraw, wqkv)):
                sp.dma_start(dst, src).then_inc(S["weights_in"], 16)
            for b in range(2):
                sp.dma_start(dR[0:NLB, b, :], dright[0:NLB, :]).then_inc(S["dstat_in"], 16)
                sp.dma_start(dR[NLB + NSEL:DROWS, b, :], dright[NLB + NSEL:DROWS, :]).then_inc(S["dstat_in"], 16)
            sp.dma_start(dL[NLB:DROWS, :, :], dleft.unsqueeze(1).broadcast_to([NSEL + SUB, NCH, P])
                         ).then_inc(S["dstat_in"], 16)
            load_w(1)

            def store_parts(g):
                v = g % 4
                sp.wait_ge(S["qk_hi"], 2 * g + 2)
                sp.wait_ge(S["qk_lo"], 2 * g + 2)
                if g == 4:
                    sp.wait_ge(S["qk_out0"], 16)
                    load_stack(0, 0)
                    for b in range(2):
                        load_exponents(chunk(0, b), b)
                sp.dma_start(qk_scr[g * GRP:(g + 1) * GRP].rearrange("c k r i -> r (c k) i"),
                             parts[:, v].rearrange("p c k i -> p (c k) i")).then_inc(S[f"qk_out{v}"], 16)

            def load_stack(cs, b):
                of_chunk = qk_scr[bass.ds(cs, 1)].rearrange("o k r i -> (o k) r i")
                sp.dma_start(qk_st[b][0:2 * HD], of_chunk.rearrange("(t k) (d h) i -> (k d) t (h i)", k=2, h=H)
                             ).then_inc(S[f"st_in{b}"], 16)
                sp.dma_start(qk_st[b][2 * HD:3 * HD], of_chunk[0::3].rearrange("t (d h) i -> d t (h i)", h=H)
                             ).then_inc(S[f"st_in{b}"], 16)

            def load_exponents(cs, b):
                sp.dma_start(dR[NLB:NLB + NSEL, b, :],
                             lb_scr[:, bass.ds(cs, 1)].rearrange("p o s h i -> (p o) s (h i)")
                             ).then_inc(S[f"dr_in{b}"], 16)

            def store_exponents():
                sp.wait_ge(S["lb_parts"], 3)
                for k in range(4):
                    for p in range(3):
                        sp.dma_start(lb_scr[p, 8 * k:8 * k + 8].rearrange("c s h i -> h (c s) i"),
                                     lbS[32 * k:32 * k + H, p, :].rearrange("p (n i) -> p n i", i=SUB)
                                     ).then_inc(S["lb_moved"], 16)

            def load_exponent_rows():
                sp.wait_ge(S["lb_moved"], 16 * 12)
                for p in range(3):
                    sp.dma_start(dL[p * H:(p + 1) * H].rearrange("p c (s i) -> p (c s) i", i=SUB),
                                 lb_scr[p].rearrange("c s h i -> h (c s) i")).then_inc(S["dl_in"], 16)

            for g in range(NGRP):
                store_parts(g)
                if g == 0:
                    store_exponents()
                if g == 1:
                    load_exponent_rows()

            def load_step(i):
                for b in range(2):
                    n, c = 2 * i + b, chunk(i, b)
                    tok, cs = bass.ds(at(sp, c * P), P), at(sp, c)
                    used, products_used = at(sp, n - 1), at(sp, 2 * n - 2)
                    wait(sp, S["pe_a"], products_used)
                    wait(sp, S["pe_d"], products_used)
                    if isinstance(n, int) and n == 1:
                        for v in range(4):
                            sp.wait_ge(S[f"qk_out{v}"], 16 * (NGRP // 4))
                    if not (isinstance(n, int) and n == 0):
                        load_stack(cs, b)
                    if not (isinstance(n, int) and n < 2):
                        load_exponents(cs, b)
                    if isinstance(n, int) and n == 0:
                        sp.wait_ge(S["lb_moved"], 16 * 12)
                        sp.wait_ge(S["qk_f32"], 2 * NGRP)
                    wait(sp, S["pe_i"], used)
                    sp.dma_start(q_now[:, b, :], qT[:, tok]).then_inc(S[f"q_in{b}"], 16)

            loop(sp, CPB, load_step)

            for b in range(2):
                sp.wait_ge(S[f"scattered{b}"], 16 * CPB)
            sp.wait_ge(S["pe_a"], 2 * NCH - 2)

            def load_rows(i):
                for u in range(2):
                    n = 2 * i + u
                    tok = bass.ds(at(sp, n * P), P)
                    wait(sp, S["xs_ps"], n - 1)
                    wait(sp, S["id_copied"], n - 1)
                    sp.dma_start(xrow[:, u, :], xsort[tok, :]).then_inc(S[f"xrow_in{u}"], 16)

            load_rows(0)
            for b in range(2):
                sp.wait_ge(S[f"q_in{b}"], 16 * CPB)
            sp.dma_start(w2_sb[:, 1:E], w2[:, 1:E]).then_inc(S["w2_in"], 16)
            loop(sp, NBLK // 2, load_rows, peel=0, start=1)

            for u in range(2):
                sp.wait_ge(S[f"y_out{u}"], 16 * (NBLK // 2))
            token_rows = [t[0:TOK].rearrange("(c p) d -> p c d", p=P) for t in (ytok, out)]
            for q in range(NQ):
                sp.dma_start(yt[:, share(q)], token_rows[0][:, share(q)]).then_inc(S[f"yt_in{q}"], 16)
            for q in range(NQ):
                sp.wait_ge(S["dve_out"], (q + 1) * NCH // NQ)
                sp.dma_start(token_rows[1][:, share(q)], yt[:, share(q)]).then_inc(S["stored"], 16)
            sp.wait_ge(S["stored"], 16 * NQ)

        @block.gpsimd
        def _(pool):
            pool.memset(zero, 0.0).then_inc(S["pool_init"], 1)
            pool.iota(rows[:, :, D].bitcast(I32), pattern=[[P, NCH]], base=0, channel_multiplier=1
                      ).then_inc(S["pool_init"], 1)
            pool.wait_ge(S["pool_init"], 2)
            pool.iota(zero[:, :, D].bitcast(I32), pattern=[[1, NBLK]], base=TOK, channel_multiplier=NBLK
                      ).then_inc(S["pool_init"], 1)
            pool.wait_ge(S["pool_init"], 3)

            def low(i):
                for u in range(2):
                    g = 2 * i + u
                    cols = bass.ds(g * GRP * P, GRP * P)
                    pool.wait_ge(S["xnT_sb"], g + 1)
                    pool.wait_ge(S["xh_ready"], g + 1)
                    pool.tensor_tensor(xl[:, cols], xnT[:, u, :], xh[:, cols], ALU.subtract).then_inc(S["xl_ready"], 1)

            loop(pool, NGRP // 2, low)
            pool.dma_start(xsort.rearrange("(p n) r -> p n r", n=NBLK), zero).then_inc(S["init_out"], 16)

            pool.wait_ge(S["lbT_sb"], 1)
            pool.wait_ge(S["tot_ps"], 1)
            for p in range(2):
                pool.wait_ge(S["lb_parts"], p + 1)
                pool.tensor_tensor(lbT, lbT, lbS[:, p, :], ALU.subtract).then_inc(S["lb_rest"], 1)

            def low_parts():
                def group(i):
                    for v in range(4):
                        g = 4 * i + v
                        cols = bass.ds(g * GRP * P, GRP * P)
                        wait(pool, S[f"qk_out{v}"], 16 * i)
                        for t, src in ((0, qT[:, cols]), (1, kT[:, v, :])):
                            pool.wait_ge(S["qk_hi"], 2 * g + 1 + t)
                            pool.tensor_tensor(parts[:, v, :, 1 + t, :], src.rearrange("p (c i) -> p c i", i=P),
                                               parts[:, v, :, 3 * t, :], ALU.subtract).then_inc(S["qk_lo"], 1)

                loop(pool, NGRP // 4, group)

            pool.wait_ge(S["const_in"], 16 * NCONSTDMA)
            pool.wait_ge(S["init_out"], 16)
            pool.wait_ge(S["slots"], 1)
            low_parts()
            pool.wait_ge(S["decays"], 3)
            pool.wait_ge(S["k2_ready"], NGRP)
            pool.wait_ge(S["v_ready"], NGRP)
            pool.wait_ge(S["lb_moved"], 16 * 12)
            pool.wait_ge(S["qk_hi"], 2 * NGRP)
            pool.wait_ge(S["qk_lo"], 2 * NGRP)

            def scatter(n):
                b, c = n % 2, chunk(n // 2, n % 2)
                wait(pool, S[f"scattered{b}"], 16 * (n // 2))
                pool.indirect_dma_start(xsort, bass.IndirectOffsetOnAxis(ap=slot_i[:, c:c + 1], axis=0),
                                        rows[:, c, :], None).then_inc(S[f"scattered{b}"], 16)

            for n in range(NCH):
                b, c = n % 2, chunk(n // 2, n % 2)
                wait(pool, S["pe_u"], n - 1)
                pool.tensor_tensor(kd[:, b, :].rearrange("p (d h) -> p d h", h=H),
                                   k2[:, c, :].rearrange("p (d h) -> p d h", h=H),
                                   sdec[:, c, :].unsqueeze(1).broadcast_to([P, HD, H]),
                                   ALU.mult).then_inc(S["pool_kd"], 1)
                wait(pool, S["pe_av"], n - 1)
                pool.tensor_tensor(v2[:, b, :].rearrange("p (h s e) -> p h s e", s=NS, e=HD),
                                   v_sb[:, c, :].rearrange("p (h e) -> p h e", e=HD).unsqueeze(2)
                                   .broadcast_to([P, H, NS, HD]),
                                   cc("smask").unsqueeze(1).unsqueeze(3).broadcast_to([P, H, NS, HD]),
                                   ALU.mult).then_inc(S["pool_v2"], 1)
                for k in range(n + LEAD if n else 0, min(n + LEAD + 1, NCH)):
                    scatter(k)

            for n in range(NBLK):
                pool.wait_ge(S["y_sb"], n + 1)
                pool.wait_ge(S["id_copied"], n + 1)
                pool.indirect_dma_start(ytok, bass.IndirectOffsetOnAxis(ap=ids[:, n:n + 1], axis=0),
                                        ysb[:, n % 2, :], None).then_inc(S[f"y_out{n % 2}"], 16)
                c = n - LEAD
                if c == 0:
                    pool.wait_ge(S["rms"], 1)
                if 0 <= c < NCH:
                    pool.tensor_scalar(attn[:, c, :], attn[:, c, :], rstd[:, c:c + 1], None, ALU.mult
                                       ).then_inc(S["pool_attn"], 1)
                    pool.wait_ge(S["pool_attn"], c + 1)
                    pool.tensor_tensor(x_sb[:, c, :], x_sb[:, c, :], attn[:, c, :], ALU.add).then_inc(S["x_done"], 1)

        @block.scalar
        def _(act):
            for dst, src in ((kept_cst[:], const[:, 0:NKEPT]), (wrf_sb[:], wrf), (early_cst, const[:, NKEPT:NCONST]),
                             (delta_sb[:], delta.partition_broadcast(P))):
                act.dma_start(dst, src).then_inc(S["const_in"], 16)

            act.wait_ge(S["eps_set"], 3)

            def deviation(g):
                gs = slice(g * GRP, (g + 1) * GRP)
                act.wait_ge(S["ln_aggr"], g + 1)
                act.activation(sdv[:, gs], mean_var[:, g % 2, :, 1], ACT.Sqrt, bias=eps_ln).then_inc(S["ln_sd"], 1)

            deviation(0)
            for g in range(NGRP):
                u = g % 2
                if g + 1 < NGRP:
                    deviation(g + 1)
                act.wait_ge(S["xnT_ps"], g + 1)
                wait(act, S["logits_ready"], g - 1)
                wait(act, S["xl_ready"], g - 1)
                act.activation(xnT[:, u, :], PS[:, u, :], ACT.Copy).then_inc(S["xnT_sb"], 1)
                act.activation(xh[:, g * GRP * P:(g + 1) * GRP * P], PS[:, u, :], ACT.Copy).then_inc(S["xh_ready"], 1)
                act.wait_ge(S[f"stage_in{g % 4}"], 16 * (g // 4) + 16)
                act.activation(w13h[:, g, :, 0, :], wstage[:, g % 4, :, :], ACT.Copy, scale=WS).then_inc(S["w_hi"], 1)

            act.wait_ge(S["weights_in"], 16 * 4)
            act.activation(wqh[:], wraw.rearrange("p w d -> p (w d)"), ACT.Copy, scale=WS).then_inc(S["wq_hi"], 1)

            act.wait_ge(S["forget_abs"], 1)
            act.activation(ze, ze, ACT.Exp).then_inc(S["forget_exp"], 1)
            act.wait_ge(S["router_in"], 1)
            act.activation(rexp, rl, ACT.Exp).then_inc(S["router_exp"], 1)
            act.wait_ge(S["forget_exp"], 1)
            act.activation(ze, ze, ACT.Ln, bias=one).then_inc(S["forget_ln"], 1)
            act.wait_ge(S["lbT_ps"], 1)
            act.activation(lbT, PS[:, 0:2, :].rearrange("p b n -> p (b n)"), ACT.Copy).then_inc(S["lbT_sb"], 1)
            act.wait_ge(S["lbT_sb"], 1)
            act.activation(lbS[:, 0, :], lbT, ACT.Copy).then_inc(S["lb_parts"], 1)
            act.wait_ge(S["cum_ps"], 1)
            act.activation(elb[:].rearrange("p c h -> p (c h)"), PS[:, 5, :], ACT.Exp).then_inc(S["decays"], 1)
            act.activation(sdec[:].rearrange("p c h -> p (c h)"), PS[:, 6, :], ACT.Exp).then_inc(S["decays"], 1)
            act.wait_ge(S["tot_ps"], 1)
            act.activation(dec[:].rearrange("p (k n) -> p k n", k=4), PS[:, 0:4, 0:NCH * NS // 4], ACT.Exp
                           ).then_inc(S["decays"], 1)

            def exponent_part(p):
                act.wait_ge(S["lb_rest"], p)
                act.activation(lbS[:, p, :], lbT, ACT.Copy).then_inc(S["lb_parts"], 1)

            exponent_part(1)

            def project(i):
                for v in range(4):
                    g, u = 4 * i + v, v % 2
                    if isinstance(i, int) and g == 1:
                        exponent_part(2)
                    act.wait_ge(S["q_ps"], g + 1)
                    act.activation(qT[:, bass.ds(g * GRP * P, GRP * P)], PS[:, 4 * u, :], ACT.Tanh, scale=0.5 / WS)
                    wait(act, S["qk_hi"], 2 * g - 6)
                    wait(act, S["qk_lo"], 2 * g - 6)
                    act.activation(kT[:, v, :], PS[:, 4 * u + 1, :], ACT.Tanh, scale=0.5 / WS).then_inc(S["qk_tanh"], 1)
                    act.wait_ge(S["kv_ps"], g + 1)
                    kv = PS[:, 4 * u + 2:4 * u + 4, :].rearrange("p b (c n) -> p b c n", n=2 * D)
                    of_group = bass.ds(g * GRP, GRP)
                    act.activation(k2[:, of_group, :].rearrange("p (b c) d -> p b c d", c=2), kv[:, :, :, 0:D], ACT.Tanh,
                                   scale=0.5 / WS).then_inc(S["k_tanh"], 1)
                    act.activation(v_sb[:, of_group, :].rearrange("p (b c) d -> p b c d", c=2),
                                   kv[:, :, :, D:2 * D], ACT.Copy).then_inc(S["v_ready"], 1)

            act.wait_ge(S["xl_ready"], NGRP)
            act.wait_ge(S["init_out"], 16)
            act.wait_ge(S["w_lo"], E)
            act.wait_ge(S["wo_ready"], 1)
            act.wait_ge(S["slots"], 1)
            act.wait_ge(S["blocks_known"], 1)
            loop(act, NGRP // 4, project)

            def attend(i):
                for b in range(2):
                    n = 2 * i + b
                    known = isinstance(n, int)

                    def has(k):
                        return not known or 0 <= n - k < NCH

                    def decays(half):
                        act.wait_ge(S["pe_d"], 2 * n + half + 1)
                        wait(act, S["dve_p"], 2 * n + half - 1)
                        act.activation(ebuf[:, half, :], PS[:, 0, :], ACT.Exp).then_inc(S["act_e"], 1)

                    if has(0):
                        decays(0)
                    if has(3):
                        u = (b - 3) % 2
                        act.wait_ge(S["pe_w"], n - 2)
                        act.wait_ge(S[f"scattered{u}"], 16 * (i + (b - 3) // 2) + 16)
                        act.activation(attn[:, bass.ds(chunk(i, b, 3), 1), :].rearrange("p o d -> p (o d)"),
                                       PS[:, 6 + u, 256:384], ACT.Copy).then_inc(S["act_attn"], 1)
                    if has(0):
                        decays(1)
                        act.wait_ge(S["g_a"], n + 1)
                        wait(act, S["g_y"], n - 1)
                        act.activation(hid0[:, b, :], PS[:, 2, :], ACT.Tanh, scale=0.5 / WS).then_inc(S["g_tanh"], 1)
                    if has(2):
                        wait(act, S["act_ss"], n - 3)
                        act.wait_ge(S["dve_o"], n - 1)
                        act.activation(squares[:, b, :], o_sb[:, b, :], ACT.Square,
                                       accum_out=ssq[:, bass.ds(chunk(i, b, 2), 1)]).then_inc(S["act_ss"], 1)
                        act.wait_ge(S["pe_t"], n - 1)
                        wait(act, S["pe_w"], n - 3)
                        act.activation(oT[:, b, :], PS[:, 4 + b, 384:512], ACT.Copy).then_inc(S["act_ot"], 1)

            act.wait_ge(S["lb_moved"], 16 * 12)
            act.wait_ge(S["qk_lo"], 2 * NGRP)
            act.wait_ge(S["k2_ready"], NGRP)

            def sorted_hi(n, u):
                act.wait_ge(S["xs_ps"], n + 1)
                wait(act, S["f_b"], n - 1)
                wait(act, S["xs_lo"], n - 1)
                act.activation(xsh[:, u, :], PS[:, u, 0:P], ACT.Copy).then_inc(S["xs_hi"], 1)

            loop(act, CPB, attend, peel=2)
            sorted_hi(0, 0)
            sorted_hi(1, 1)
            attend(CPB)
            act.wait_ge(S["pe_w"], NCH)
            act.wait_ge(S["scattered1"], 16 * CPB)
            act.activation(attn[:, NCH - 1, :], PS[:, 7, 256:384], ACT.Copy).then_inc(S["act_attn"], 1)

            def silu_of(n, u):
                act.wait_ge(S["f_a"], n + 1)
                wait(act, S["f_h"], n - 1)
                act.activation(silu[:, u, :], PS[:, 2 + 4 * u, :], ACT.Silu, scale=1.0 / WS).then_inc(S["f_silu"], 1)

            def y_copy(n, u, turn):
                act.wait_ge(S["f_y"], n + 1)
                wait(act, S[f"y_out{u}"], 16 * turn)
                act.activation(ysb[:, u, :], PS[:, 4 + u, 0:D], ACT.Copy).then_inc(S["y_sb"], 1)

            def routed(i):
                for v in range(2):
                    n, u = 2 * i + 1 + v, (1 + v) % 2
                    sorted_hi(n + 1, 1 - u)
                    silu_of(n, u)
                    y_copy(n - 1, 1 - u, i)

            act.wait_ge(S["dve_p"], 2 * NCH)
            silu_of(0, 0)
            routed(0)
            act.wait_ge(S["act_ss"], NCH)
            act.activation(sdv, ssq, ACT.Sqrt, scale=1.0 / D, bias=eps_rms).then_inc(S["rms_sd"], 1)
            loop(act, NBLK // 2 - 1, routed, start=1)
            silu_of(NBLK - 1, 1)
            y_copy(NBLK - 2, 0, NBLK // 2 - 1)
            y_copy(NBLK - 1, 1, NBLK // 2 - 1)

        @block.vector
        def _(dve):
            count = {}

            def link(ins, name):
                count[name] = count.get(name, 0) + 1
                ins.then_inc(S[name], 1)
                dve.wait_ge(S[name], count[name])

            dve.memset(eps_ln, LN_EPS).then_inc(S["eps_set"], 1)
            dve.memset(eps_rms, RMS_EPS * OS * OS).then_inc(S["eps_set"], 1)
            dve.memset(one, 1.0).then_inc(S["eps_set"], 1)
            dve.memset(lf[:, NCH * H:], 0.0)

            assert NGRP == E

            def statistics(g):
                u = g % 2
                dve.wait_ge(S[f"x_in{g % 4}"], 16 * (g // 4) + 16)
                wait(dve, S["ln_aggr"], g - 1)
                for j in range(GRP):
                    last = dve.bn_stats(stats[:, u, j, :], x_sb[:, g * GRP + j, :])
                last.then_inc(S["ln_stats"], 1)
                dve.wait_ge(S["ln_stats"], g + 1)
                wait(dve, S["xn_ready"], g - 1)
                wait(dve, S["ln_sd"], g - 1)
                for j in range(GRP):
                    last = dve.bn_aggr(mean_var[:, u, j, :], stats[:, u, j, :])
                last.then_inc(S["ln_aggr"], 1)

            def low_w(e):
                dve.wait_ge(S["w_hi"], e + 1)
                dve.scalar_tensor_tensor(w13h[:, e, :, 1, :], wstage[:, e % 4, :, :], WS, w13h[:, e, :, 0, :],
                                         ALU.mult, ALU.subtract).then_inc(S["w_lo"], 1)

            statistics(0)
            for g in range(NGRP):
                u = g % 2
                gs = slice(g * GRP, (g + 1) * GRP)
                if g + 1 < NGRP:
                    statistics(g + 1)
                dve.wait_ge(S["ln_sd"], g + 1)
                dve.reciprocal(rstd[:, gs], sdv[:, gs]).then_inc(S["ln_rstd"], 1)
                dve.wait_ge(S["ln_rstd"], g + 1)
                for j in range(GRP):
                    c = g * GRP + j
                    last = dve.tensor_scalar(rows[:, c, 0:D], x_sb[:, c, :], mean_var[:, u, j, 0:1], rstd[:, c:c + 1],
                                             ALU.subtract, ALU.mult)
                last.then_inc(S["xn_ready"], 1)
                if g > 0:
                    low_w(g - 1)
            low_w(E - 1)

            dve.wait_ge(S["logits_ready"], NGRP)
            dve.wait_ge(S["const_in"], 16 * NCONSTDMA)
            link(dve.tensor_tensor(zf, lg[:, :, E:E + H],
                                   delta_sb[:].unsqueeze(1).broadcast_to([P, NCH, H]), ALU.add), "forget")
            link(dve.tensor_scalar(zm, zf, 0.0, None, ALU.min), "forget")
            dve.scalar_tensor_tensor(ze, zm, 2.0, zf, ALU.mult, ALU.subtract).then_inc(S["forget_abs"], 1)
            link(dve.tensor_copy(rl, lg[:, :, 0:E]), "router")
            link(dve.tensor_reduce(rmax, rl, AX_X, ALU.max), "router")
            dve.tensor_tensor(rl, rl, rmax.unsqueeze(2).broadcast_to([P, NCH, E]), ALU.subtract).then_inc(S["router_in"], 1)
            dve.wait_ge(S["router_exp"], 1)
            dve.tensor_reduce(rsum, rexp, AX_X, ALU.add)
            link(dve.tensor_reduce(ptop, rexp[:, :, 1:E], AX_X, ALU.max), "router")
            dve.tensor_tensor(eq, rexp[:, :, 1:E], ptop.unsqueeze(2).broadcast_to([P, NCH, R]), ALU.is_equal)
            dve.wait_ge(S["forget_ln"], 1)
            dve.tensor_tensor(lf[:, 0:NCH * H], zm.rearrange("p c h -> p (c h)"), ze.rearrange("p c h -> p (c h)"),
                              ALU.subtract).then_inc(S["lf_ready"], 1)
            link(dve.tensor_tensor(den, rexp[:, :, 0], ptop, ALU.add), "router")
            link(dve.scalar_tensor_tensor(den2, rsum, 1e-9, den, ALU.mult, ALU.max), "router")
            link(dve.reciprocal(den, den2), "router")
            dve.scalar_tensor_tensor(g0, rexp[:, :, 0], 0.5 / (WS * WS), den, ALU.mult, ALU.mult).then_inc(S["gates"], 1)
            dve.scalar_tensor_tensor(g1, ptop, 1.0 / WS, den, ALU.mult, ALU.mult).then_inc(S["gates"], 1)
            link(dve.tensor_tensor(eq, eq, cc("order").unsqueeze(1).broadcast_to([P, NCH, R]), ALU.mult), "router")
            link(dve.tensor_reduce(oscore, eq, AX_X, ALU.max), "router")
            dve.tensor_tensor(oh, eq, oscore.unsqueeze(2).broadcast_to([P, NCH, R]), ALU.is_equal).then_inc(S["onehot"], 1)
            dve.wait_ge(S["wq_hi"], 1)
            dve.wait_ge(S["weights_in"], 16 * 4)
            dve.scalar_tensor_tensor(wql[:], wraw.rearrange("p w d -> p (w d)"), WS, wqh[:],
                                     ALU.mult, ALU.subtract).then_inc(S["wq_lo"], 1)
            dve.tensor_scalar(wo_sb[:], wo_raw, nw_sb[:, 0:1], None, ALU.mult).then_inc(S["wo_ready"], 1)
            dve.wait_ge(S["rank_ps"], 1)
            link(dve.tensor_copy(tt, ntok_ps), "router")
            link(dve.tensor_tensor_scan(incl.rearrange("p e c -> p (e c)"), cc("scan0"),
                                        tt.rearrange("p e c -> p (e c)"), 0.0, ALU.mult, ALU.add), "router")
            link(dve.tensor_tensor(off, incl[:, :, NCH - 1:NCH].broadcast_to([P, R, NCH]),
                                   cc("fill").unsqueeze(1).broadcast_to([P, R, NCH]), ALU.is_gt), "router")
            link(dve.tensor_reduce(nblk[:, 0, :], off, AX_X, ALU.add), "router")
            link(dve.tensor_tensor_scan(nblk[:, 1, :], cc("one7"), nblk[:, 0, :], 0.0, ALU.mult, ALU.add), "router")
            link(dve.tensor_tensor(nblk[:, 2, :], nblk[:, 1, :], nblk[:, 0, :], ALU.subtract), "router")
            link(dve.tensor_tensor(off, incl, tt, ALU.subtract), "router")
            link(dve.scalar_tensor_tensor(off, nblk[:, 2, :].unsqueeze(2).broadcast_to([P, R, NCH]), float(P), off,
                                          ALU.mult, ALU.add), "router")
            link(dve.tensor_tensor(eq, rank_ps, off.rearrange("p e c -> p c e"), ALU.add), "router")
            link(dve.tensor_tensor(eq, eq, oh, ALU.mult), "router")
            link(dve.tensor_reduce(slot, eq, AX_X, ALU.add), "router")
            dve.tensor_copy(slot_i[:], slot).then_inc(S["slots"], 1)
            link(dve.tensor_tensor(bcmp, cc("blk")[0:1].unsqueeze(2).broadcast_to([1, NBLK, R - 1]),
                                   nblk[0:1, 1, 0:R - 1].unsqueeze(1).broadcast_to([1, NBLK, R - 1]), ALU.is_ge), "router")
            link(dve.tensor_reduce(bsum, bcmp, AX_X, ALU.add), "router")
            dve.tensor_scalar(expert[:], bsum, 1.0, None, ALU.add).then_inc(S["blocks_known"], 1)

            dve.wait_ge(S["w_lo"], E)
            dve.wait_ge(S["slots"], 1)
            dve.wait_ge(S["blocks_known"], 1)
            dve.wait_ge(S["xl_ready"], NGRP)
            dve.wait_ge(S["init_out"], 16)

            def gate(i):
                for v in range(4):
                    g, u = 4 * i + v, v % 2
                    cols = bass.ds(g * GRP * P, GRP * P)
                    dve.wait_ge(S["qk_tanh"], g + 1)
                    for t, dst in ((0, qT[:, cols]), (1, kT[:, v, :])):
                        dve.scalar_tensor_tensor(dst, dst, 1.0, PS[:, 4 * u + t, :], ALU.add, ALU.mult
                                                 ).then_inc(S["qk_f32"], 1)
                    dve.wait_ge(S["qk_f32"], 2 * g + 2)
                    wait(dve, S[f"qk_out{v}"], 16 * i)
                    for t, src in ((0, qT[:, cols]), (1, kT[:, v, :])):
                        dve.tensor_copy(parts[:, v, :, 3 * t, :], src.rearrange("p (c i) -> p c i", i=P)
                                        ).then_inc(S["qk_hi"], 1)
                    dve.wait_ge(S["k_tanh"], g + 1)
                    dve.wait_ge(S["v_ready"], g + 1)
                    kv = PS[:, 4 * u + 2:4 * u + 4, :].rearrange("p b (c n) -> p b c n", n=2 * D)
                    keys = k2[:, bass.ds(g * GRP, GRP), :].rearrange("p (b c) d -> p b c d", c=2)
                    dve.scalar_tensor_tensor(keys, keys, 1.0, kv[:, :, :, 0:D], ALU.add, ALU.mult
                                             ).then_inc(S["k2_ready"], 1)

            loop(dve, NGRP // 4, gate)

            dve.wait_ge(S["lb_moved"], 16 * 12)
            dve.wait_ge(S["decays"], 3)
            dve.wait_ge(S["gates"], 2)
            dve.wait_ge(S["qk_lo"], 2 * NGRP)
            link(dve.memset(state[:, :, 0, :], 0.0), "state_zero")

            def finish(i, b):
                n = 2 * i + b
                u, c = (b - 1) % 2, chunk(i, b, 1)
                dve.wait_ge(S["pe_i"], n)
                dve.wait_ge(S["dve_s1"], n)
                dve.scalar_tensor_tensor(state[:, u, 0, :], state[:, u, 1, :], dec[:, bass.ds(c * NS + 1, 1)],
                                         um[:, u, 1, :], ALU.mult, ALU.add).then_inc(S["dve_s0"], 1)
                dve.wait_ge(S["pe_av"], n)
                wait(dve, S["dve_o"], n - 1)
                dve.tensor_tensor(o1.rearrange("p (h d) -> p h d", d=HD),
                                  PS[:, 4 + u, 256:384].rearrange("p (h d) -> p h d", d=HD),
                                  elb[:, bass.ds(c, 1), :].rearrange("p o h -> p (o h)").unsqueeze(2).broadcast_to([P, H, HD]),
                                  ALU.mult).then_inc(S["dve_o1"], 1)
                dve.wait_ge(S["dve_o1"], n)
                wait(dve, S["pe_t"], n - 2)
                wait(dve, S["act_ss"], n - 2)
                av = PS[0:SUB, 4 + u, 0:2 * D].rearrange("p (h s e) -> p h s e", s=NS, e=HD)
                for s in range(NS):
                    tok = slice(s * SUB, (s + 1) * SUB)
                    last = dve.tensor_tensor(o_sb[tok, u, :].rearrange("p (h e) -> p h e", e=HD),
                                             o1[tok, :].rearrange("p (h e) -> p h e", e=HD),
                                             av[:, :, s, :], ALU.add)
                last.then_inc(S["dve_o"], 1)
                dve.wait_ge(S["g_y"], n)
                cx = bass.ds(n - 1, 1)
                x_rows = x_sb[:, cx, :].rearrange("p o d -> p (o d)")
                dve.scalar_tensor_tensor(x_rows, PS[:, 6 + u, 384:512], g0[:, cx], x_rows,
                                         ALU.mult, ALU.add).then_inc(S["dve_y"], 1)

            def attend(i):
                for b in range(2):
                    n, c = 2 * i + b, chunk(i, b)
                    for half in range(2):
                        dve.wait_ge(S["act_e"], 2 * n + half + 1)
                        dve.wait_ge(S["pe_a"], 2 * n + half + 1)
                        wait(dve, S["pe_av"], n - 1)
                        if isinstance(n, int) and n == 0:
                            for v in range(2):
                                dve.wait_ge(S[f"qk_out{v}"], 16 * (NGRP // 4))
                        dve.tensor_tensor(pbuf[:, b, half * 512:(half + 1) * 512], ebuf[:, half, :], PS[:, 1, :],
                                          ALU.mult).then_inc(S["dve_p"], 1)
                    dve.wait_ge(S["g_tanh"], n + 1)
                    dve.scalar_tensor_tensor(hid0[:, b, :], hid0[:, b, :], 1.0, PS[:, 2, :], ALU.add, ALU.mult
                                             ).then_inc(S["g_silu"], 1)
                    dve.wait_ge(S["g_silu"], n + 1)
                    dve.wait_ge(S["g_b"], n + 1)
                    dve.tensor_tensor(hid0[:, b, :], hid0[:, b, :], PS[:, 3, :], ALU.mult).then_inc(S["g_h"], 1)
                    dve.wait_ge(S["pe_u"], n + 1)
                    wait(dve, S["dve_s0"], n - 1)
                    dve.tensor_tensor(um[:, b].rearrange("p s (h e) -> p s h e", e=HD),
                                      PS[:, 6 + b, 0:2 * D].rearrange("p (h s e) -> p s h e", s=NS, e=HD),
                                      cc("hmask").unsqueeze(1).unsqueeze(3).broadcast_to([P, NS, H, HD]),
                                      ALU.mult).then_inc(S["dve_um"], 1)
                    dve.wait_ge(S["dve_um"], n + 1)
                    wait(dve, S["pe_i"], n - 1)
                    dve.scalar_tensor_tensor(state[:, b, 1, :], state[:, b, 0, :], dec[:, bass.ds(c * NS, 1)],
                                             um[:, b, 0, :], ALU.mult, ALU.add).then_inc(S["dve_s1"], 1)
                    if not (isinstance(n, int) and n == 0):
                        finish(i, b)

            def sorted_lo(n, u, turn):
                dve.wait_ge(S[f"xrow_in{u}"], 16 * turn + 16)
                dve.tensor_copy(ids[:, bass.ds(n, 1)], xrow[:, u, D:ROW].bitcast(I32)).then_inc(S["id_copied"], 1)
                dve.wait_ge(S["xs_hi"], n + 1)
                wait(dve, S["f_b"], n - 1)
                dve.tensor_tensor(xsl[:, u, :], PS[:, u, 0:P], xsh[:, u, :], ALU.subtract).then_inc(S["xs_lo"], 1)

            loop(dve, CPB, attend, peel=2)
            sorted_lo(0, 0, 0)
            sorted_lo(1, 1, 0)
            finish(CPB, 0)

            def hidden(n, u):
                dve.wait_ge(S["f_silu"], n + 1)
                dve.wait_ge(S["f_b"], n + 1)
                wait(dve, S["f_y"], n - 1)
                dve.tensor_tensor(hid[:, u, :], silu[:, u, :], PS[:, 3 + 4 * u, :], ALU.mult).then_inc(S["f_h"], 1)

            def routed(i):
                for v in range(2):
                    n, u = 2 * i + 1 + v, (1 + v) % 2
                    sorted_lo(n + 1, 1 - u, i + 1)
                    hidden(n, u)

            hidden(0, 0)
            routed(0)
            dve.wait_ge(S["rms_sd"], 1)
            dve.reciprocal(rstd, sdv).then_inc(S["rms"], 1)
            loop(dve, NBLK // 2 - 1, routed, peel=0, start=1)
            hidden(NBLK - 1, 1)

            dve.wait_ge(S["x_done"], NCH)
            for q in range(NQ):
                dve.wait_ge(S[f"yt_in{q}"], 16)
                for c in range(NCH)[share(q)]:
                    dve.scalar_tensor_tensor(yt[:, c, :], yt[:, c, :], g1[:, c:c + 1], x_sb[:, c, :],
                                             ALU.mult, ALU.add).then_inc(S["dve_out"], 1)

        @block.tensor
        def _(pe):
            def mm(out_, lhsT, rhs, start=True, stop=True):
                return pe.matmul(out_, lhsT, rhs, start=start, stop=stop)

            def split_product(out_, a_hi, a_lo, b_hi, b_lo):
                mm(out_, a_hi, b_hi, True, False)
                mm(out_, a_hi, b_lo, False, False)
                return mm(out_, a_lo, b_hi, False, True)

            pe.wait_ge(S["const_in"], 16 * NCONSTDMA)

            for g in range(NGRP):
                u = g % 2
                pe.wait_ge(S["xn_ready"], g + 1)
                wait(pe, S["xh_ready"], g - 1)
                for j in range(GRP):
                    last = pe.transpose(PS[:, u, j * P:(j + 1) * P], rows[:, g * GRP + j, 0:D], cc("ident"))
                last.then_inc(S["xnT_ps"], 1)
                pe.wait_ge(S["xnT_sb"], g + 1)
                for j in range(GRP):
                    last = mm(lg[:, g * GRP + j, 0:E + H], xnT[:, u, j * P:(j + 1) * P], wrf_sb[:])
                last.then_inc(S["logits_ready"], 1)

            pe.wait_ge(S["lf_ready"], 1)
            pe.wait_ge(S["xh_ready"], NGRP)
            for c in range(NCH):
                k, col = c // 8, (c % 8) * P
                last = mm(PS[32 * k:32 * k + 32, col // 512, col % 512:col % 512 + P],
                          lf[:, c * H:c * H + 32], cc("cum"))
            last.then_inc(S["lbT_ps"], 1)
            pe.wait_ge(S["onehot"], 1)
            flat = oh.rearrange("p c e -> p (c e)")
            mm(PS[:, 4, 0:NCH * R], cc("rank"), flat)
            mm(PS[:, 4, NCH * R:2 * NCH * R], cc("ones"), flat).then_inc(S["rank_ps"], 1)
            flat = lf[:, 0:NCH * H]
            mm(PS[:, 5, :], cc("cum"), flat)
            mm(PS[:, 6, :], cc("suffix"), flat).then_inc(S["cum_ps"], 1)
            pe.wait_ge(S["lbT_sb"], 1)
            pe.wait_ge(S["router_in"], 1)
            for k in range(4):
                rows_k = slice(32 * k, 32 * k + H)
                last = mm(PS[:, k, 0:NCH * NS // 4], cc("expand")[rows_k],
                          lbT[rows_k, :].rearrange("p (n i) -> p n i", i=SUB)[:, :, SUB - 1])
            last.then_inc(S["tot_ps"], 1)

            pe.wait_ge(S["decays"], 3)
            pe.wait_ge(S["wq_lo"], 1)
            pe.wait_ge(S["xl_ready"], NGRP)

            def project(i):
                for u in range(2):
                    g = 2 * i + u
                    cols = bass.ds(g * GRP * P, GRP * P)
                    if isinstance(g, int) and g == 1:
                        pe.wait_ge(S["slots"], 1)
                    wait(pe, S["qk_f32"], 2 * g - 2)
                    for t in range(2):
                        w = slice(t * D, (t + 1) * D)
                        last = split_product(PS[:, 4 * u + t, :], wqh[:, w], wql[:, w], xh[:, cols], xl[:, cols])
                    last.then_inc(S["q_ps"], 1)
                    wait(pe, S["k2_ready"], g - 1)
                    wait(pe, S["v_ready"], g - 1)
                    for j in range(GRP):
                        tok = bass.ds(g * GRP * P + j * P, P)
                        last = split_product(PS[:, 4 * u + 2 + j // 2, (j % 2) * 2 * D:(j % 2 + 1) * 2 * D],
                                             xh[:, tok], xl[:, tok], wqh[:, D:3 * D], wql[:, D:3 * D])
                    last.then_inc(S["kv_ps"], 1)

            loop(pe, NGRP // 2, project)

            def up(e, w, bank, hi, lo):
                for f in range(FB):
                    cols = slice(f * P, (f + 1) * P)
                    wt = [w13h[:, bass.ds(e, 1), w, part, cols].rearrange("p o f -> p (o f)") for part in range(2)]
                    last = split_product(PS[:, bank, cols], wt[0], wt[1], hi, lo)
                return last

            def down(weights, hidden, out_):
                for f in range(FB):
                    last = mm(out_, hidden[:, f * P:(f + 1) * P], weights[:, f, :], f == 0, f == FB - 1)
                return last

            pe.wait_ge(S["w_lo"], E)
            pe.wait_ge(S["qk_f32"], 2 * NGRP)
            pe.wait_ge(S["k2_ready"], NGRP)
            pe.wait_ge(S["v_ready"], NGRP)
            pe.wait_ge(S["dstat_in"], 16 * 5)
            pe.wait_ge(S["dl_in"], 16 * 3)
            pe.wait_ge(S["weights_in"], 16 * 4)
            pe.wait_ge(S["wo_ready"], 1)
            pe.wait_ge(S["state_zero"], 1)

            def step(i, b):
                n = 2 * i + b
                known = isinstance(n, int)

                def has(k):
                    return not known or 0 <= n - k < NCH

                u = 1 - b
                if has(0):
                    def weights(half):
                        pe.wait_ge(S[f"dr_in{b}"], 16 * i + 16)
                        wait(pe, S["act_e"], 2 * n + half)
                        mm(PS[:, 0, :], dL[:, bass.ds(chunk(i, b), 1), :].rearrange("p o t -> p (o t)"),
                           dR[:, b, half * 512:(half + 1) * 512]).then_inc(S["pe_d"], 1)
                        pe.wait_ge(S[f"st_in{b}"], 32 * i + 32)
                        wait(pe, S["dve_p"], 2 * n + half)
                        for h in range(half * H // 2, (half + 1) * H // 2):
                            for s in range(NS):
                                sub = slice(s * SUB, (s + 1) * SUB)
                                tok = slice(h * P + s * SUB, h * P + (s + 1) * SUB)
                                last = mm(PS[sub, 1, (h % 8) * SUB:(h % 8 + 1) * SUB],
                                          qk_st[b][:, 1, tok], qk_st[b][:, 0, tok])
                        last.then_inc(S["pe_a"], 1)

                    weights(0)
                    tok = bass.ds(n * P, P)
                    wait(pe, S["g_silu"], n)
                    up(0, 0, 2, xh[:, tok], xl[:, tok]).then_inc(S["g_a"], 1)
                    wait(pe, S["g_h"], n)
                    up(0, 1, 3, xh[:, tok], xl[:, tok]).then_inc(S["g_b"], 1)
                    weights(1)
                if has(2):
                    pe.wait_ge(S["dve_o"], n - 1)
                    wait(pe, S["act_ot"], n - 3)
                    pe.transpose(PS[:, 4 + b, 384:512], o_sb[:, b, :], cc("ident")).then_inc(S["pe_t"], 1)
                if has(0):
                    pe.wait_ge(S["pool_kd"], n + 1)
                    pe.wait_ge(S["pool_v2"], n + 1)
                    wait(pe, S["dve_um"], n - 1)
                    wait(pe, S["act_attn"], n - 3)
                    wait(pe, S["dve_y"], n - 1)
                    mm(PS[:, 6 + b, 0:2 * D], kd[:, b, :], v2[:, b, :]).then_inc(S["pe_u"], 1)
                if has(1):
                    pe.wait_ge(S["dve_s1"], n)
                    wait(pe, S["dve_s0"], n - 2)
                    wait(pe, S["dve_o"], n - 2)
                    wait(pe, S["act_ot"], n - 2)
                    pe.wait_ge(S[f"q_in{u}"], 16 * (i + (b - 1) // 2) + 16)
                    for s in range(NS):
                        tok = slice(s * SUB, (s + 1) * SUB)
                        last = mm(PS[tok, 4 + u, 256:384], q_now[:, u, tok], state[:, u, s, :])
                    last.then_inc(S["pe_i"], 1)
                    pe.wait_ge(S["dve_p"], 2 * n)
                    for h in range(H):
                        last = mm(PS[0:SUB, 4 + u, h * NS * HD:(h + 1) * NS * HD],
                                  pbuf[:, u, h * SUB:(h + 1) * SUB], v2[:, u, h * NS * HD:(h + 1) * NS * HD])
                    last.then_inc(S["pe_av"], 1)
                    pe.wait_ge(S["g_h"], n)
                    wait(pe, S["act_attn"], n - 2)
                    down(w2_first[:], hid0[:, u, :], PS[:, 6 + u, 384:512]).then_inc(S["g_y"], 1)
                if has(2):
                    pe.wait_ge(S["act_ot"], n - 1)
                    pe.wait_ge(S["dve_um"], min(n + 1, NCH) if known else n + 1)
                    pe.wait_ge(S["dve_y"], n - 1)
                    mm(PS[:, 6 + b, 256:384], oT[:, b, :], wo_sb[:]).then_inc(S["pe_w"], 1)

            def attend(i):
                for b in range(2):
                    step(i, b)

            def turn_rows(n, u, turn):
                pe.wait_ge(S[f"xrow_in{u}"], 16 * turn + 16)
                wait(pe, S["xs_lo"], n - 1)
                pe.transpose(PS[:, u, 0:P], xrow[:, u, 0:D], cc("ident")).then_inc(S["xs_ps"], 1)

            UNROLL = 12
            block_expert = [pe.alloc_register(f"block_expert{k}") for k in range(UNROLL + 1)]

            def experts_of(n, count):
                pe.load(block_expert[:count], expert[0:1, bass.ds(n, count)])
                return [pe.snap(reg, min_val=1, max_val=E - 1) for reg in block_expert[:count]]

            def up_routed(n, u, e):
                pe.wait_ge(S["xs_hi"], n + 1)
                pe.wait_ge(S["xs_lo"], n + 1)
                wait(pe, S["f_silu"], n - 1)
                wait(pe, S["f_h"], n - 1)
                for w in range(2):
                    up(e, w, 2 + 4 * u + w, xsh[:, u, :], xsl[:, u, :]).then_inc(S["f_" + "ab"[w]], 1)

            def down_routed(n, u, e):
                pe.wait_ge(S["f_h"], n + 1)
                wait(pe, S["y_sb"], n - 1)
                down(w2_sb[:, bass.ds(e, 1)].rearrange("p o f d -> p (o f) d"), hid[:, u, :], PS[:, 4 + u, 0:D]
                     ).then_inc(S["f_y"], 1)

            loop(pe, CPB, attend, peel=2)

            pe.wait_ge(S["act_e"], 2 * NCH)
            pe.wait_ge(S["dve_p"], 2 * NCH)
            turn_rows(0, 0, 0)
            turn_rows(1, 1, 0)
            step(CPB, 0)
            pe.wait_ge(S["g_h"], NCH)
            up_routed(0, 0, experts_of(0, 1)[0])
            step(CPB, 1)
            pe.wait_ge(S["act_attn"], NCH)
            pe.wait_ge(S["dve_y"], NCH)
            pe.wait_ge(S["w2_in"], 16)

            def routed(i):
                for v in range(UNROLL):
                    n, u = UNROLL * i + 1 + v, (1 + v) % 2
                    turn_rows(n + 1, 1 - u, UNROLL // 2 * i + (v + 2) // 2)
                    if v == 0:
                        e = experts_of(UNROLL * i, UNROLL + 1)
                    up_routed(n, u, e[v + 1])
                    down_routed(n - 1, 1 - u, e[v])

            assert (NBLK - 2) % UNROLL == 0
            loop(pe, (NBLK - 2) // UNROLL, routed)
            e = experts_of(NBLK - 2, 2)
            up_routed(NBLK - 1, 1, e[1])
            down_routed(NBLK - 2, 0, e[0])
            down_routed(NBLK - 1, 1, e[1])


def kernel(L0_attn_x, L0_attn_Wq, L0_attn_Wk, L0_attn_Wv, L0_attn_Wo, L0_attn_Wf, L0_attn_delta,
           L0_attn_norm_weight, L0_ffn_Wr, L0_ffn_W1, L0_ffn_W2, L0_ffn_W3):
    import concourse.bacc as bacc
    from concourse.bass_utils import run_bass_kernel_spmd

    dleft, dright = decay_constants()
    arrays = {
        "x": np.ascontiguousarray(L0_attn_x).reshape(TOK, D),
        "wqkv": np.ascontiguousarray(np.stack(
            [np.asarray(w).reshape(H, HD, D).transpose(1, 0, 2).reshape(D, D).T for w in (L0_attn_Wq, L0_attn_Wk)]
            + [np.asarray(L0_attn_Wv).T], 1)),
        "wo": np.ascontiguousarray(np.asarray(L0_attn_Wo).T),
        "wrf": np.ascontiguousarray(np.concatenate([np.asarray(L0_ffn_Wr), np.asarray(L0_attn_Wf)], 0).T),
        "delta": np.ascontiguousarray(L0_attn_delta),
        "nw": np.ascontiguousarray(L0_attn_norm_weight).reshape(D, 1),
        "w13": np.ascontiguousarray(np.stack([np.asarray(L0_ffn_W1), np.asarray(L0_ffn_W3)], 1).transpose(3, 0, 1, 2)),
        "w2": np.ascontiguousarray(np.asarray(L0_ffn_W2).reshape(E, D, FB, P).transpose(3, 0, 2, 1)),
        "const": constants(),
        "dleft": dleft,
        "dright": dright,
    }
    nc = bacc.Bacc("TRN2", target_bir_lowering=False, num_devices=1)
    args = [nc.dram_tensor(n, a.shape, mybir.dt.from_np(a.dtype), kind="ExternalInput").ap() for n, a in arrays.items()]
    args.append(nc.dram_tensor("out", (TOK, D), F32, kind="ExternalOutput").ap())
    for n, shape, dt in (("qk_scr", (NCH, 4, D, P), F16), ("lb_scr", (3, NCH, NS, H, SUB), BF16),
                         ("xsort", (NBLK * P, ROW), F32), ("ytok", (TOK + NBLK * P, D), F32)):
        args.append(nc.dram_tensor(n, shape, dt, kind="Internal").ap())
    build(nc, *args)
    r = run_bass_kernel_spmd(nc, [arrays], core_ids=[0])
    return np.asarray(r.results[0]["out"]).reshape(BATCH, SEQ, D)
```
